# Optimizing a Trainium2 kernel written in Bass

```python
import numpy as np
import jax
import jax.numpy as jnp

def _softmax(x, axis=-1):
    return jax.nn.softmax(x, axis=axis)
def _gelu(x):
    return jax.nn.gelu(x, approximate=True)
def _silu(x):
    return jax.nn.silu(x)
def _sigmoid(x):
    return jax.nn.sigmoid(x)
def _layernorm(x, axis=-1, eps=1e-5):
    m = jnp.mean(x, axis=axis, keepdims=True)
    v = jnp.var(x, axis=axis, keepdims=True)
    return (x - m) / jnp.sqrt(v + eps)
def _scatter_add(tgt, idx, src, axis=0):
    return tgt.at[idx].add(src)
def _segment_sum(src, seg, n):
    return jax.ops.segment_sum(src, seg, n)

kernel_name = 'mk_conv_seq_d1_conv_nchw512_015edc'

def setup_inputs(seed: int = 0):
    np.random.seed(seed)
    _w = jnp.asarray
    def _rec_inputs():
        import jax
        import jax.numpy as jnp
        _gk = jax.random.key(seed)
        x = -9.26e-05 + 0.9999 * jax.random.normal(jax.random.fold_in(_gk, 1), (8, 512, 96, 96), jnp.float32)
        return x
    x = _rec_inputs()
    def _L0_conv_setup():
        import jax, jax.numpy as jnp
        import numpy as np
        N, C, H, W = (8, 512, 96, 96)
        CQK = C // 8
        NEG = -1e+30
        key = jax.random.key(seed)
        ks = jax.random.split(key, 8)
        s = 0.02
        return {'x': jax.random.normal(ks[0], (N, C, H, W), dtype=jnp.float32), 'wq': jax.random.normal(ks[1], (CQK, C), dtype=jnp.float32) * s, 'bq': jax.random.normal(ks[2], (CQK,), dtype=jnp.float32) * s, 'wk': jax.random.normal(ks[3], (CQK, C), dtype=jnp.float32) * s, 'bk': jax.random.normal(ks[4], (CQK,), dtype=jnp.float32) * s, 'wv': jax.random.normal(ks[5], (C, C), dtype=jnp.float32) * s, 'bv': jax.random.normal(ks[6], (C,), dtype=jnp.float32) * s, 'gamma': jnp.float32(0.5)}
    _L0_conv_all = _L0_conv_setup()
    _L0_conv_in = {k: v for k, v in _L0_conv_all.items() if k in ('wq', 'bq', 'wk', 'bk', 'wv', 'bv', 'gamma', )}
    del _L0_conv_all

    return {
        "x": x,
        "L0_conv_wq": _L0_conv_in["wq"],
        "L0_conv_bq": _L0_conv_in["bq"],
        "L0_conv_wk": _L0_conv_in["wk"],
        "L0_conv_bk": _L0_conv_in["bk"],
        "L0_conv_wv": _L0_conv_in["wv"],
        "L0_conv_bv": _L0_conv_in["bv"],
        "L0_conv_gamma": _L0_conv_in["gamma"],
    }

def reference(x, L0_conv_wq, L0_conv_bq, L0_conv_wk, L0_conv_bk, L0_conv_wv, L0_conv_bv, L0_conv_gamma):
    import jax
    import jax.numpy as jnp
    def _L0_conv_ref(x, wq, bq, wk, bk, wv, bv, gamma):
        import jax, jax.numpy as jnp
        import numpy as np
        N, C, H, W = (8, 512, 96, 96)
        CQK = C // 8
        NEG = -1e+30
        q = jnp.einsum('nchw,oc->nohw', x, wq) + bq[None, :, None, None]
        k = jnp.einsum('nchw,oc->nohw', x, wk) + bk[None, :, None, None]
        v = jnp.einsum('nchw,oc->nohw', x, wv) + bv[None, :, None, None]
        h, w = (q.shape[2], q.shape[3])
        e_row = jnp.einsum('ncyx,ncyi->niyx', q, k)
        e_col = jnp.einsum('ncyx,ncix->niyx', q, k)
        diag = jnp.eye(h, dtype=bool)[None, :, :, None]
        e_col = jnp.where(diag, NEG, e_col)
        energy = jnp.concatenate([e_row, e_col], axis=1)
        attn = jax.nn.softmax(energy, axis=1)
        a_row, a_col = (attn[:, :w], attn[:, w:])
        out = jnp.einsum('niyx,ncyi->ncyx', a_row, v) + jnp.einsum('niyx,ncix->ncyx', a_col, v)
        return gamma * out + x

    def _gn(v, G=32, eps=1e-5):
        B_, C_, H_, W_ = v.shape
        g = v.reshape(B_, G, C_ // G, H_, W_)
        m = jnp.mean(g, axis=(2, 3, 4), keepdims=True)
        s = jnp.var(g, axis=(2, 3, 4), keepdims=True)
        return ((g - m) / jnp.sqrt(s + eps)).reshape(v.shape)

    def _ln_c(v, eps=1e-6):
        m = jnp.mean(v, axis=1, keepdims=True)
        s = jnp.var(v, axis=1, keepdims=True)
        return (v - m) / jnp.sqrt(s + eps)

    def _ln_t(v, eps=1e-5):
        m = jnp.mean(v, axis=-1, keepdims=True)
        s = jnp.var(v, axis=-1, keepdims=True)
        return (v - m) / jnp.sqrt(s + eps)

    def _to_tokens(v):
        B_, C_, H_, W_ = v.shape
        return v.reshape(B_, C_, H_ * W_).transpose(0, 2, 1)
    def _from_tokens(t, like):
        B_, C_, H_, W_ = like.shape
        return t.transpose(0, 2, 1).reshape(B_, C_, H_, W_)

    x = _L0_conv_ref(x, L0_conv_wq, L0_conv_bq, L0_conv_wk, L0_conv_bk, L0_conv_wv, L0_conv_bv, L0_conv_gamma)
    return x


_drawn_inputs = setup_inputs


def setup_inputs(seed=0):
    import zlib

    import numpy as np

    out = dict(_drawn_inputs(seed))
    spreads = {}
    factors = {'L0_conv_bq': 8.0, 'L0_conv_bk': 8.0, 'L0_conv_bv': 5.513}
    for name, (base, spread) in spreads.items():
        noise = np.random.default_rng([zlib.crc32(name.encode()), seed]).standard_normal(out[name].shape)
        drawn = base * np.exp(spread * noise) if base else spread * noise
        out[name] = jnp.asarray(drawn.astype(out[name].dtype))
    for name, factor in factors.items():
        out[name] = (out[name] * factor).astype(out[name].dtype)
    return out
```

```python
from contextlib import ExitStack

import concourse.bass as bass
from concourse import mybir

F32 = mybir.dt.float32
F32R = mybir.dt.float32r
F16 = mybir.dt.float16
BF16 = mybir.dt.bfloat16
U32 = mybir.dt.uint32
ALU = mybir.AluOpType
ACT = mybir.ActivationFunctionType
AX = mybir.AxisListType

P = 128
N, C, H, W = 8, 512, 96, 96
CQ = C // 8
S = 96
CH = C // P
L = 4
BL = L * S
NB = S // L
PX = H * W
XR = 4
CP = XR * 4
NP = P // CP
KEPT = 2
SPILT = CH - KEPT
NEG = -1e30
P_SCALE = 4096.0
X_SCALE = 4096.0
TINY = 2.0 ** -100
EXPONENT = 0x7F800000


def walk(eng, step, tail):
    for t in range(XR):
        step(t, t)
    with eng.Fori(1, NB // XR) as j:
        for u in range(XR):
            step(j * XR + u, XR + u)
    for t in range(NB, NB + tail):
        step(t, t)


def inside(k):
    return 0 <= k < NB


def criss_cross(nc, x, wqkT, bqk, wvT, bv, gamma, out):
    ctx = ExitStack()
    with ctx:
        def sb(name, shape, dt):
            return ctx.enter_context(nc.sbuf_tensor(name, shape, dt))

        def sem(name):
            return ctx.enter_context(nc.semaphore(name))

        row_exp_dram = nc.dram_tensor("row_exp_dram", (S, NB, BL), F32, kind="Internal").ap()
        spill_dram = nc.dram_tensor("spill_dram", (SPILT, P, PX), F32, kind="Internal").ap()

        x_rows = x.rearrange("n (c p) (b l) w -> n b p c (l w)", p=P, l=L)
        out_rows = out.rearrange("n (c p) (b l) w -> n b p c (l w)", p=P, l=L)
        x_cols = x.rearrange("n (g c) y w -> n g y c w", c=CP)

        wv_hi = sb("wv_hi", [P, CH, C], F32R)
        wv_lo = sb("wv_lo", [P, CH, C], F32R)
        wqk_hi = sb("wqk_hi", [P, CH, P], F32R)
        wqk_lo = sb("wqk_lo", [P, CH, P], F32R)
        ident = sb("ident", [P, P], F32)
        ident_bf = sb("ident_bf", [S, S], BF16)
        neg_diag = sb("neg_diag", [S, L, S], BF16)
        bqk_sb = sb("bqk_sb", [P, 1], F32)
        gamma_sb = sb("gamma_sb", [P, 1], F32)
        bv_sb = sb("bv_sb", [P, CH], F32)
        gbv = sb("gbv", [P, CH], F32)
        x_ring = sb("x_ring", [P, XR, CH * BL], F32)
        x_amax = sb("x_amax", [P, NB], F32)
        scale_sb = sb("scale_sb", [P, 8], F32)
        amax1, amax_all, x_scale, x_unscale, power = (scale_sb[:, i:i + 1] for i in range(5))
        neg_max = sb("neg_max", [S, 2, L], F32)
        exp_sum = sb("exp_sum", [S, 2, L], F32)
        row_nmax = sb("row_nmax", [S, S], F32)
        row_sum = sb("row_sum", [S, S], F32)
        col_nmax = sb("col_nmax", [S, S], F32)
        col_sum = sb("col_sum", [S, S], F32)
        row_factor = sb("row_factor", [S, S], F32)
        col_factor = sb("col_factor", [S, S], F32)
        weight = sb("weight", [S, 2, BL], F32)

        kept = sb("kept", [P, KEPT, PX], F32)
        qk_all = kept[:, 0, :]
        col_exp = kept[0:S, 1, :]
        LOWER = 2 * PX * 2 // 4
        UPPER = 2 * S * P * 2 // 4
        area = sb("area", [P, LOWER + UPPER], F32)

        AREA = nc.lookup_mloc(area).addr

        def part(at, name, shape, dt, parts=P):
            return nc.alloc_sbuf_tensor_at(name, [parts, *shape], dt, offset=AREA + 4 * at)

        HALF = CH * BL
        xr_hi = [part(i * HALF, f"xr_hi{i}", [CH, BL], F32R) for i in range(2)]
        xr_lo = [part((2 + i) * HALF, f"xr_lo{i}", [CH, BL], F32R) for i in range(2)]
        row_exp = [part(4 * HALF + i * BL, f"row_exp{i}", [L, S], F32, S) for i in range(4)]
        assert 4 * HALF + 4 * BL <= LOWER
        qk = [part(LOWER + i * BL, f"qk{i}", [BL], F32) for i in range(2)]
        k_low = [part(LOWER + (2 + i) * BL, f"k_low{i}", [BL], F32, CQ) for i in range(2)]
        colw_hi = part(0, "colw_hi", [S, S], F16, S)
        colw_lo = part(PX // 2, "colw_lo", [S, S], F16, S)
        xc_hi = part(LOWER, "xc_hi", [S, P], F16, S)
        xc_lo = part(LOWER + UPPER // 2, "xc_lo", [S, P], F16, S)
        T16 = L * C // 2
        xt_hi = [part(i * T16, f"xt_hi{i}", [L, C], F16, S) for i in range(2)]
        xt_lo = [part((2 + i) * T16, f"xt_lo{i}", [L, C], F16, S) for i in range(2)]
        at = 4 * T16
        av_hi = [part(at + i * HALF, f"av_hi{i}", [CH, BL], F32R) for i in range(2)]
        at += 2 * HALF
        av_lo = [part(at + i * HALF, f"av_lo{i}", [CH, BL], F32R) for i in range(2)]
        at += 2 * HALF
        av = part(at, "av", [CH, BL], F32)
        at += HALF
        spill_in = [part(at + i * SPILT * BL, f"spill_in{i}", [SPILT, BL], F32) for i in range(2)]
        at += 2 * SPILT * BL
        row_exp_in = [part(at + i * BL, f"row_exp_in{i}", [BL], F32, S) for i in range(2)]
        at += 2 * BL
        roww_hi = [part(at + i * BL // 2, f"roww_hi{i}", [BL], F16, S) for i in range(2)]
        at += BL
        roww_lo = [part(at + i * BL // 2, f"roww_lo{i}", [BL], F16, S) for i in range(2)]
        at += BL
        assert at <= LOWER + UPPER

        bank = [ctx.enter_context(nc.psum_tensor(f"bank{i}", [P, 512], F32)) for i in range(8)]
        qk_ps = [bank[0][:, 0:BL], bank[1][:, 0:BL]]
        e_ps = [bank[2][0:S, 0:BL], bank[3][0:S, 0:BL]]
        stat_ps = bank[4][0:S, 0:2 * S]
        factor_ps = bank[5][0:S, 0:S]
        colw_ps = [bank[6][0:S, 0:BL], bank[7][0:S, 0:BL]]
        col_ps = [bank[i][:, 0:BL] for i in range(4)]
        xt_ps = [bank[4][0:S, :], bank[5][0:S, :]]
        roww_ps = bank[6][0:S, 0:BL]
        row_ps = [bank[0][:, 0:BL], bank[1][:, 0:BL]]
        v_ps = [bank[2][:, 0:BL], bank[3][:, 0:BL]]

        SEED = 1
        s_const = sem("const_loaded")
        s_gamma = sem("gamma_loaded")
        s_id0 = sem("ident_cleared")
        s_id = sem("ident_ready")
        s_gbv = sem("gamma_bv_ready")
        s_whi = sem("weights_hi_ready")
        s_wlo = sem("weights_lo_ready")
        s_xin = [sem(f"x_loaded{i}") for i in range(XR)]
        s_xhi = sem("xr_hi_ready")
        s_xlo = sem("xr_lo_ready")
        s_amax = sem("x_amax_ready")
        s_qk = sem("qk_projected")
        s_qkev = sem("qk_evacuated")
        s_big = sem("qk_kept")
        s_colqk = sem("qk_column_ready")
        s_klow = sem("k_low_ready")
        s_e = sem("energy_ready")
        s_nmax = sem("neg_max_ready")
        s_exp = sem("exp_ready")
        s_stat = sem("stats_kept")
        s_passed = sem("waits_passed")
        s_mkept = sem("neg_max_kept")
        s_rstore = [sem(f"row_exp_stored{i}") for i in range(XR)]
        s_sall = sem("amax_all_ready")
        s_statT = sem("col_stats_transposed")
        s_dve = sem("dve_chain")
        s_fexp = sem("factor_exp_ready")
        s_fT = sem("col_factor_transposed")
        s_colf = sem("col_factor_ready")
        s_cw = sem("col_weight_ready")
        s_cwT = sem("col_weight_transposed")
        s_cwhi = sem("colw_hi_ready")
        s_cwlo = sem("colw_lo_ready")
        s_xchi = sem("xc_hi_ready")
        s_xclo = sem("xc_lo_ready")
        s_col = sem("col_average_ready")
        s_evA = sem("col_average_even_kept")
        s_evD = sem("col_average_odd_kept")
        s_spill = [sem(f"col_average_spilt{g}") for g in range(SPILT)]
        s_spin = [sem(f"spill_loaded{i}") for i in range(2)]
        s_rin = [sem(f"row_exp_loaded{i}") for i in range(2)]
        s_rw = sem("row_weight_ready")
        s_rwT = sem("row_weight_transposed")
        s_rwhi = sem("roww_hi_ready")
        s_rwlo = sem("roww_lo_ready")
        s_xT = sem("x_transposed")
        s_xthi = sem("xt_hi_ready")
        s_xtlo = sem("xt_lo_ready")
        s_row = sem("row_average_ready")
        s_av = sem("average_ready")
        s_avhi = sem("av_hi_ready")
        s_avlo = sem("av_lo_ready")
        s_v = sem("value_ready")
        s_out = sem("output_ready")
        s_store = [sem(f"output_stored{i}") for i in range(XR)]

        AMAX_AT, SCALE_AT, MAX_AT, COL_FACTOR_AT, CHAIN = 1, 6, 10, 16, 17

        XPI = 2 * NB + CH * NP
        LPS = XPI // XR

        def x_loaded(eng, n, first, b, k):
            eng.wait_ge(s_xin[k % XR], 16 * (n * LPS + first // XR + (b - k % XR) // XR + 1)
                        if isinstance(b, int) else (n * LPS + first // XR + 1) * 16 + (b - k % XR) * (16 // XR))

        def slot_stored(eng, sems, n, b, k):
            eng.wait_ge(sems[k % XR], 16 * SEED + n * (16 * NB // XR) + (b - k % XR) * (16 // XR))

        def all_stored(eng, sems, n):
            for s in sems:
                eng.wait_ge(s, 16 * SEED + n * (16 * NB // XR))

        def alone(eng):
            eng.sem_inc(s_passed, 1)

        block = ctx.enter_context(nc.Block())

        @block.sync
        def _(sp):
            sp.dma_start(gamma_sb[:, :], gamma).then_inc(s_gamma, 16)
            sp.dma_start(x_ring[:, 0:2, :].rearrange("p s n -> p (s n)")[:, 0:CH * C].rearrange("p (c n) -> p c n", c=CH),
                         wvT.rearrange("(c p) n -> p c n", p=P)).then_inc(s_const, 16)
            sp.dma_start(x_ring[:, 2, 0:CH * P].rearrange("p (c n) -> p c n", c=CH),
                         wqkT.rearrange("(c p) n -> p c n", p=P)).then_inc(s_const, 16)
            sp.dma_start(bqk_sb[:, :], bqk).then_inc(s_const, 16)
            sp.dma_start(bv_sb[:, :], bv).then_inc(s_const, 16)
            for s in (*s_rstore, *s_store):
                sp.sem_inc(s, 16 * SEED)
            sp.wait_ge(s_wlo, 2)
            with sp.Fori(0, N) as n:
                def rows_step(t, k):
                    if inside(k):
                        if k < XR:
                            sp.wait_ge(s_store[k], 16 * SEED + n * (16 * NB // XR))
                        else:
                            sp.wait_ge(s_xlo, n * NB + t - (XR - 1))
                            sp.wait_ge(s_amax, n * NB + t - (XR - 1))
                        sp.dma_start(x_ring[:, k % XR, :].rearrange("p (c n) -> p c n", c=CH),
                                     x_rows[n, t]).then_inc(s_xin[k % XR], 16)
                    if inside(k - 4):
                        sp.wait_ge(s_exp, n * (2 * NB) + t - 3)
                        sp.dma_start(row_exp_dram[:, t - 4, :],
                                     row_exp[k % 4][:, :, :].rearrange("p l n -> p (l n)")).then_inc(s_rstore[k % 4], 16)

                walk(sp, rows_step, 4)

                for g in range(CH):
                    for i in range(NP):
                        if g == 0 and i < XR:
                            sp.wait_ge(s_xlo, (n + 1) * NB)
                            sp.wait_ge(s_amax, (n + 1) * NB)
                        else:
                            sp.wait_ge(s_xclo, n * (CH * NP) + g * NP + i - (XR - 1))
                        sp.dma_start(x_ring[0:S, i % XR, :].rearrange("p (c n) -> p c n", c=CP),
                                     x_cols[n, g * NP + i]).then_inc(s_xin[i % XR], 16)
                    if 1 <= g <= SPILT:
                        sp.wait_ge(s_evA, SEED + n * (CH * NB // 2) + g * (NB // 2))
                        sp.wait_ge(s_evD, SEED + n * (CH * NB // 2) + g * (NB // 2))
                        sp.dma_start(spill_dram[g - 1], kept[:, (g - 1) % KEPT, :]).then_inc(s_spill[g - 1], 16)

                def out_step(t, k):
                    if inside(k):
                        if k == 0:
                            sp.wait_ge(s_col, SEED + (n + 1) * (CH * NB))
                            alone(sp)
                            for g in range(SPILT):
                                sp.wait_ge(s_spill[g], n * 16 + 16)
                                alone(sp)
                            all_stored(sp, s_rstore, n + 1)
                            alone(sp)
                        if k < XR:
                            sp.wait_ge(s_xclo, n * (CH * NP) + CH * NP - XR + 1 + k)
                        else:
                            slot_stored(sp, s_store, n, t, k)
                        sp.dma_start(x_ring[:, k % XR, :].rearrange("p (c n) -> p c n", c=CH),
                                     x_rows[n, t]).then_inc(s_xin[k % XR], 16)
                        if k >= 2:
                            sp.wait_ge(s_rw, n * NB + t - 1)
                            alone(sp)
                        sp.dma_start(row_exp_in[k % 2][:, :], row_exp_dram[:, t, :]).then_inc(s_rin[k % 2], 16)
                        if k >= 2:
                            sp.wait_ge(s_av, n * (CH * NB) + t * CH - CH)
                        sp.dma_start(spill_in[k % 2][:, :, :], spill_dram.rearrange("c p (b n) -> b p c n", n=BL)[t])\
                            .then_inc(s_spin[k % 2], 16)
                    if inside(k - 3):
                        sp.wait_ge(s_out, n * (CH * NB) + t * CH - 2 * CH)
                        sp.dma_start(out_rows[n, t - 3],
                                     x_ring[:, (k - 3) % XR, :].rearrange("p (c n) -> p c n", c=CH))\
                            .then_inc(s_store[(k - 3) % XR], 16)

                walk(sp, out_step, 3)
            all_stored(sp, s_store, N)

        @block.gpsimd
        def _(pool):
            pool.memset(ident[:, :], 0.0).then_inc(s_id0, 1)
            pool.memset(ident_bf[:, :], 0.0).then_inc(s_id0, 1)
            pool.memset(neg_diag[:, :, :], 0.0).then_inc(s_id0, 1)
            pool.wait_ge(s_id0, 3)
            pool.affine_select(out=ident[:, :], in_=ident[:, :], compare_op=ALU.not_equal, fill=1.0, base=0,
                               pattern=[[-1, P]], channel_multiplier=1).then_inc(s_id, 1)
            pool.affine_select(out=ident_bf[:, :], in_=ident_bf[:, :], compare_op=ALU.not_equal, fill=1.0, base=0,
                               pattern=[[-1, S]], channel_multiplier=1).then_inc(s_id, 1)
            pool.affine_select(out=neg_diag[:, :, :], in_=neg_diag[:, :, :], compare_op=ALU.not_equal, fill=NEG,
                               base=0, pattern=[[0, L], [-1, S]], channel_multiplier=1).then_inc(s_id, 1)
            with pool.Fori(0, N) as n:
                def rows_step(t, k):
                    if inside(k):
                        x_loaded(pool, n, 0, t, k)
                        pool.wait_ge(s_xhi, n * NB + t + 1)
                        pool.tensor_tensor(xr_lo[k % 2][:, :, :].rearrange("p c n -> p (c n)"), x_ring[:, k % XR, :],
                                           xr_hi[k % 2][:, :, :].rearrange("p c n -> p (c n)").bitcast(F32),
                                           ALU.subtract).then_inc(s_xlo, 1)
                    if inside(k - 1):
                        pool.wait_ge(s_qkev, n * NB + t)
                        alone(pool)
                        pool.tensor_copy(qk_all[:, bass.ds((t - 1) * BL, BL)], qk[(k - 1) % 2][:, :]).then_inc(s_big, 1)

                walk(pool, rows_step, 1)

                qk_by_col = qk_all.rearrange("p (y x) -> p x y", x=S)
                pool.wait_ge(s_big, (n + 1) * NB)

                def cols_step(t, k):
                    pool.wait_ge(s_e, n * (2 * NB) + NB + t - 1)
                    alone(pool)
                    pool.tensor_copy(qk[k % 2][:, :].rearrange("p (l y) -> p l y", l=L),
                                     qk_by_col[:, bass.ds(t * L, L), :]).then_inc(s_colqk, 1)

                walk(pool, cols_step, 0)

                pool.wait_ge(s_dve, n * CHAIN + AMAX_AT)
                alone(pool)
                pool.partition_all_reduce(amax_all, amax1, P, bass.bass_isa.ReduceOp.max).then_inc(s_sall, 1)

                pool.wait_ge(s_colf, n + 1)
                col_exp3 = col_exp.rearrange("p (x y) -> p x y", y=S)

                def colw_step(t, k):
                    if k >= 2:
                        pool.wait_ge(s_cwT, n * NB + t - 1)
                    pool.tensor_tensor(weight[:, k % 2, :].rearrange("p (l n) -> p l n", l=L),
                                       col_exp3[:, bass.ds(t * L, L), :],
                                       col_factor[:, bass.ds(t * L, L)].unsqueeze(2).to_broadcast([S, L, S]),
                                       ALU.mult).then_inc(s_cw, 1)

                walk(pool, colw_step, 0)

                pool.wait_ge(s_dve, (n + 1) * CHAIN)

                def out_step(t, k):
                    if inside(k):
                        pool.wait_ge(s_rin[k % 2], n * (8 * NB) + (t - k % 2) * 8 + 16)
                        if k >= 2:
                            pool.wait_ge(s_rwT, n * NB + t - 1)
                        else:
                            pool.wait_ge(s_cwT, (n + 1) * NB)
                        pool.tensor_tensor(weight[:, k % 2, :].rearrange("p (l n) -> p l n", l=L),
                                           row_exp_in[k % 2][:, :].rearrange("p (l n) -> p l n", l=L),
                                           row_factor[:, bass.ds(t * L, L)].unsqueeze(2).to_broadcast([S, L, S]),
                                           ALU.mult).then_inc(s_rw, 1)
                    if inside(k - 2):
                        for c in range(CH):
                            pool.wait_ge(s_avhi, n * (CH * NB) + (t - 2) * CH + c + 1)
                            pool.tensor_tensor(av_lo[k % 2][:, c, :], av[:, c, :],
                                               av_hi[k % 2][:, c, :].bitcast(F32), ALU.subtract).then_inc(s_avlo, 1)

                walk(pool, out_step, 2)

        @block.scalar
        def _(act):
            act.wait_ge(s_gamma, 16)
            act.wait_ge(s_const, 64)
            wv_in = x_ring[:, 0:2, :].rearrange("p s n -> p (s n)")[:, 0:CH * C].rearrange("p (c n) -> p c n", c=CH)
            wqk_in = x_ring[:, 2, 0:CH * P].rearrange("p (c n) -> p c n", c=CH)
            act.activation(wv_hi[:, :, :], wv_in, ACT.Copy, scale=gamma_sb[:, 0:1]).then_inc(s_whi, 1)
            act.activation(wqk_hi[:, :, :], wqk_in, ACT.Copy).then_inc(s_whi, 1)
            with act.Fori(0, N) as n:
                def exps(t, k, first, dest):
                    act.wait_ge(s_nmax, n * (2 * NB) + first + t + 1)
                    for r in range(L):
                        last = act.activation(dest[:, r, :], e_ps[k % 2][:, r * S:(r + 1) * S], ACT.Exp,
                                              bias=neg_max[:, k % 2, r:r + 1], accum_out=exp_sum[:, k % 2, r:r + 1])
                    last.then_inc(s_exp, 1)

                def rows_step(t, k):
                    if inside(k):
                        x_loaded(act, n, 0, t, k)
                        if k >= 2:
                            act.wait_ge(s_qk, n * NB + t - 1)
                        elif k == 0:
                            act.wait_ge(s_v, SEED + n * (CH * NB))
                        act.activation(xr_hi[k % 2][:, :, :].rearrange("p c n -> p (c n)"), x_ring[:, k % XR, :],
                                       ACT.Copy).then_inc(s_xhi, 1)
                    if inside(k - 1):
                        act.wait_ge(s_qk, n * NB + t)
                        if k - 1 >= 2:
                            act.wait_ge(s_big, n * NB + t - 2)
                            act.wait_ge(s_e, n * (2 * NB) + t - 2)
                        act.activation(qk[(k - 1) % 2][:, :], qk_ps[(k - 1) % 2], ACT.Identity,
                                       bias=bqk_sb[:, 0:1]).then_inc(s_qkev, 1)
                    if inside(k - 2):
                        if k - 2 >= 4:
                            slot_stored(act, s_rstore, n, t - 2, k - 2)
                        if k - 2 >= 2:
                            act.wait_ge(s_stat, n * (2 * NB) + t - 3)
                        exps(t - 2, k, 0, row_exp[(k - 2) % 4][:, :, :])

                walk(act, rows_step, 2)

                col_exp3 = col_exp.rearrange("p (x y) -> p x y", y=S)

                def cols_step(t, k):
                    act.wait_ge(s_stat, n * (2 * NB) + NB + t - 1)
                    exps(t, k, NB, col_exp3[:, bass.ds(t * L, L), :])

                walk(act, cols_step, 0)

                act.wait_ge(s_dve, n * CHAIN + MAX_AT)
                act.activation(row_nmax[:, :], row_nmax[:, :], ACT.Exp).then_inc(s_fexp, 1)
                act.activation(row_factor[:, :], row_factor[:, :], ACT.Exp).then_inc(s_fexp, 1)

                all_stored(act, s_rstore, n + 1)

                def colw_step(t, k):
                    act.wait_ge(s_cwT, n * NB + t + 1)
                    act.activation(colw_hi[:, bass.ds(t * L, L), :],
                                   colw_ps[k % 2].rearrange("p (l n) -> p l n", l=L), ACT.Copy).then_inc(s_cwhi, 1)

                walk(act, colw_step, 0)

                act.wait_ge(s_dve, n * CHAIN + SCALE_AT)
                for g in range(CH):
                    act.wait_ge(s_col, SEED + n * (CH * NB) + g * NB)
                    for i in range(NP):
                        x_loaded(act, n, NB + g * NP + i - i % XR, i % XR, i)
                        act.activation(xc_hi[:, :, i * CP:(i + 1) * CP].rearrange("p x c -> p c x"),
                                       x_ring[0:S, i % XR, :].rearrange("p (c n) -> p c n", c=CP), ACT.Copy,
                                       scale=x_scale[0:S, :]).then_inc(s_xchi, 1)
                    if g >= KEPT:
                        act.wait_ge(s_spill[g - KEPT], n * 16 + 16)
                    kept_by_col = kept[:, g % KEPT, :].rearrange("p (y x) -> p x y", x=S)
                    with act.Fori(0, NB // 4) as j:
                        for u in (0, 2):
                            act.wait_ge(s_col, SEED + n * (CH * NB) + g * NB + j * 4 + u + 1)
                            act.activation(kept_by_col[:, bass.ds(j * (4 * L) + u * L, L), :],
                                           col_ps[u].rearrange("p (l n) -> p l n", l=L), ACT.Copy,
                                           scale=x_unscale).then_inc(s_evA, 1)

                def out_step(t, k):
                    if inside(k):
                        act.wait_ge(s_rwT, n * NB + t + 1)
                        if k >= 2:
                            act.wait_ge(s_row, n * (CH * NB) + t * CH - CH)
                        elif k == 0:
                            act.wait_ge(s_col, SEED + (n + 1) * (CH * NB))
                        act.activation(roww_hi[k % 2][:, :], roww_ps, ACT.Copy).then_inc(s_rwhi, 1)
                    for r in range(4):
                        if inside(k):
                            act.wait_ge(s_xT, n * (L * NB) + t * L + r + 1)
                            act.activation(xt_hi[k % 2][:, r, :], xt_ps[r % 2], ACT.Copy,
                                           scale=x_scale[0:S, :]).then_inc(s_xthi, 1)
                        if inside(k - 1):
                            act.wait_ge(s_av, n * (CH * NB) + (t - 1) * CH + r + 1)
                            if k - 1 >= 2 and r == 0:
                                act.wait_ge(s_v, SEED + n * (CH * NB) + (t - 2) * CH)
                            act.activation(av_hi[(k - 1) % 2][:, r, :], av[:, r, :], ACT.Copy).then_inc(s_avhi, 1)

                walk(act, out_step, 1)

        @block.vector
        def _(dve):
            wv_in = x_ring[:, 0:2, :].rearrange("p s n -> p (s n)")[:, 0:CH * C].rearrange("p (c n) -> p c n", c=CH)
            wqk_in = x_ring[:, 2, 0:CH * P].rearrange("p (c n) -> p c n", c=CH)
            dve.wait_ge(s_const, 64)
            dve.wait_ge(s_gamma, 16)
            dve.tensor_scalar(gbv[:, :], bv_sb[:, :], gamma_sb[:, 0:1], None, ALU.mult).then_inc(s_gbv, 1)
            dve.wait_ge(s_gbv, 1)
            dve.wait_ge(s_whi, 2)
            dve.scalar_tensor_tensor(out=wv_lo[:, :, :], in0=wv_in, scalar=gamma_sb[:, 0:1],
                                     in1=wv_hi[:, :, :].bitcast(F32), op0=ALU.mult,
                                     op1=ALU.subtract).then_inc(s_wlo, 1)
            dve.tensor_tensor(wqk_lo[:, :, :], wqk_in, wqk_hi[:, :, :].bitcast(F32), ALU.subtract).then_inc(s_wlo, 1)
            with dve.Fori(0, N) as n:
                def lower_k(t, k, first):
                    if k >= 2 or first:
                        dve.wait_ge(s_e, n * (2 * NB) + first + t - 1)
                    dve.tensor_copy(k_low[k % 2][:, :], qk[k % 2][CQ:2 * CQ, :]).then_inc(s_klow, 1)

                def line_max(t, k, first, matrix):
                    dve.wait_ge(s_e, n * (2 * NB) + first + t + 1)
                    if k >= 2 or first:
                        dve.wait_ge(s_exp, n * (2 * NB) + first + t - 1)
                    dve.tensor_reduce(neg_max[:, k % 2, :], e_ps[k % 2].rearrange("p (l n) -> p l n", l=L), AX.X,
                                      ALU.max, negate=True).then_inc(s_nmax, 1)
                    dve.wait_ge(s_nmax, n * (2 * NB) + first + t + 1)
                    dve.tensor_copy(matrix[:, bass.ds(t * L, L)], neg_max[:, k % 2, :]).then_inc(s_mkept, 1)

                def line_sum(t, k, first, matrix):
                    dve.wait_ge(s_exp, n * (2 * NB) + first + t + 1)
                    dve.tensor_copy(matrix[:, bass.ds(t * L, L)], exp_sum[:, k % 2, :]).then_inc(s_stat, 1)

                def rows_step(t, k):
                    if inside(k):
                        x_loaded(dve, n, 0, t, k)
                        dve.tensor_reduce(x_amax[:, bass.ds(t, 1)], x_ring[:, k % XR, :], AX.X, ALU.max,
                                          apply_absolute_value=True).then_inc(s_amax, 1)
                    if inside(k - 1):
                        dve.wait_ge(s_qkev, n * NB + t)
                        lower_k(t - 1, k - 1, 0)
                    if inside(k - 2):
                        line_max(t - 2, k - 2, 0, row_nmax)
                    if inside(k - 3):
                        line_sum(t - 3, k - 3, 0, row_sum)

                walk(dve, rows_step, 3)

                def cols_step(t, k):
                    if inside(k):
                        dve.wait_ge(s_colqk, n * NB + t + 1)
                        lower_k(t, k, NB)
                    if inside(k - 1):
                        line_max(t - 1, k - 1, NB, col_nmax)
                    if inside(k - 2):
                        line_sum(t - 2, k - 2, NB, col_sum)

                walk(dve, cols_step, 2)

                done = [0]

                def chain(ins):
                    done[0] += 1
                    ins.then_inc(s_dve, 1)
                    dve.wait_ge(s_dve, n * CHAIN + done[0])

                dve.wait_ge(s_amax, (n + 1) * NB)
                chain(dve.tensor_reduce(amax1, x_amax[:, :], AX.X, ALU.max))
                assert done[0] == AMAX_AT
                dve.wait_ge(s_sall, n + 1)
                chain(dve.tensor_scalar(amax_all, amax_all, TINY, None, ALU.max))
                chain(dve.tensor_scalar(power.bitcast(U32), amax_all.bitcast(U32), EXPONENT, None, ALU.bitwise_and))
                chain(dve.tensor_scalar(x_scale.bitcast(U32), amax_all.bitcast(U32), EXPONENT, EXPONENT,
                                        ALU.bitwise_xor, ALU.bitwise_and))
                chain(dve.tensor_scalar(x_unscale, power, 0.5 / (X_SCALE * P_SCALE), None, ALU.mult))
                chain(dve.tensor_scalar(x_scale, x_scale, X_SCALE, None, ALU.mult))
                assert done[0] == SCALE_AT

                dve.wait_ge(s_mkept, (n + 1) * (2 * NB))
                dve.wait_ge(s_stat, (n + 1) * (2 * NB))
                dve.wait_ge(s_statT, n + 1)
                joint = weight[:, 0, 0:S]
                col_sumT = weight[:, 0, S:2 * S]
                chain(dve.tensor_tensor(joint, stat_ps[:, 0:S], row_nmax[:, :], ALU.min))
                chain(dve.tensor_copy(col_sumT, stat_ps[:, S:2 * S]))
                chain(dve.tensor_tensor(row_nmax[:, :], joint, row_nmax[:, :], ALU.subtract))
                chain(dve.tensor_tensor(row_factor[:, :], joint, stat_ps[:, 0:S], ALU.subtract))
                assert done[0] == MAX_AT
                dve.wait_ge(s_fexp, 2 * n + 2)
                chain(dve.tensor_tensor(row_sum[:, :], row_sum[:, :], row_nmax[:, :], ALU.mult))
                chain(dve.tensor_tensor(col_sumT, col_sumT, row_factor[:, :], ALU.mult))
                chain(dve.tensor_tensor(joint, row_sum[:, :], col_sumT, ALU.add))
                chain(dve.reciprocal(joint, joint))
                chain(dve.tensor_scalar(joint, joint, P_SCALE, None, ALU.mult))
                chain(dve.tensor_tensor(col_sumT, row_factor[:, :], joint, ALU.mult))
                assert done[0] == COL_FACTOR_AT
                chain(dve.tensor_tensor(row_factor[:, :], row_nmax[:, :], joint, ALU.mult))
                assert done[0] == CHAIN
                dve.wait_ge(s_fT, n + 1)
                dve.tensor_copy(col_factor[:, :], factor_ps).then_inc(s_colf, 1)

                def colw_step(t, k):
                    dve.wait_ge(s_cwhi, n * NB + t + 1)
                    dve.tensor_tensor(colw_lo[:, bass.ds(t * L, L), :],
                                      colw_ps[k % 2].rearrange("p (l n) -> p l n", l=L),
                                      colw_hi[:, bass.ds(t * L, L), :], ALU.subtract).then_inc(s_cwlo, 1)

                walk(dve, colw_step, 0)

                for g in range(CH):
                    for i in range(NP):
                        dve.wait_ge(s_xchi, n * (CH * NP) + g * NP + i + 1)
                        dve.scalar_tensor_tensor(out=xc_lo[:, :, i * CP:(i + 1) * CP].rearrange("p x c -> p c x"),
                                                 in0=x_ring[0:S, i % XR, :].rearrange("p (c n) -> p c n", c=CP),
                                                 scalar=x_scale[0:S, :],
                                                 in1=xc_hi[:, :, i * CP:(i + 1) * CP].rearrange("p x c -> p c x"),
                                                 op0=ALU.mult, op1=ALU.subtract).then_inc(s_xclo, 1)
                    if g >= KEPT:
                        dve.wait_ge(s_spill[g - KEPT], n * 16 + 16)
                        alone(dve)
                    kept_by_col = kept[:, g % KEPT, :].rearrange("p (y x) -> p x y", x=S)
                    with dve.Fori(0, NB // 4) as j:
                        for u in (1, 3):
                            dve.wait_ge(s_col, SEED + n * (CH * NB) + g * NB + j * 4 + u + 1)
                            dve.tensor_scalar(kept_by_col[:, bass.ds(j * (4 * L) + u * L, L), :],
                                              col_ps[u].rearrange("p (l n) -> p l n", l=L), x_unscale, None,
                                              ALU.mult).then_inc(s_evD, 1)

                dve.wait_ge(s_evA, SEED + (n + 1) * (CH * NB // 2))

                def out_step(t, k):
                    if inside(k):
                        dve.wait_ge(s_rwhi, n * NB + t + 1)
                        dve.tensor_tensor(roww_lo[k % 2][:, :], roww_ps, roww_hi[k % 2][:, :], ALU.subtract).then_inc(s_rwlo, 1)
                    for r in range(4):
                        if inside(k):
                            dve.wait_ge(s_xthi, n * (L * NB) + t * L + r + 1)
                            dve.scalar_tensor_tensor(out=xt_lo[k % 2][:, r, :], in0=xt_ps[r % 2],
                                                     scalar=x_scale[0:S, :], in1=xt_hi[k % 2][:, r, :],
                                                     op0=ALU.mult, op1=ALU.subtract).then_inc(s_xtlo, 1)
                        if inside(k - 1):
                            dve.wait_ge(s_row, n * (CH * NB) + (t - 1) * CH + r + 1)
                            if k - 1 >= 1:
                                dve.wait_ge(s_avlo, n * (CH * NB) + (t - 2) * CH + r + 1)
                            if r < SPILT:
                                if r == 0:
                                    dve.wait_ge(s_spin[(k - 1) % 2], n * (8 * NB) + (t - 1 - (k - 1) % 2) * 8 + 16)
                                col = spill_in[(k - 1) % 2][:, r, :]
                            else:
                                col = kept[:, r % KEPT, bass.ds((t - 1) * BL, BL)]
                            dve.scalar_tensor_tensor(out=av[:, r, :], in0=row_ps[r % 2], scalar=x_unscale, in1=col,
                                                     op0=ALU.mult, op1=ALU.add).then_inc(s_av, 1)
                        if inside(k - 2):
                            dve.wait_ge(s_v, SEED + n * (CH * NB) + (t - 2) * CH + r + 1)
                            res = x_ring[:, (k - 2) % XR, r * BL:(r + 1) * BL]
                            dve.scalar_tensor_tensor(out=res, in0=v_ps[r % 2], scalar=gbv[:, r:r + 1], in1=res,
                                                     op0=ALU.add, op1=ALU.add).then_inc(s_out, 1)

                walk(dve, out_step, 2)

        @block.tensor
        def _(pe):
            for s in (s_v, s_col, s_evA, s_evD):
                pe.sem_inc(s, SEED)
            pe.wait_ge(s_id, 3)
            pe.wait_ge(s_wlo, 2)
            with pe.Fori(0, N) as n:
                def energies(t, k, first, masked):
                    pe.wait_ge(s_klow, n * (2 * NB) + first + t + 1)
                    if k >= 2 or first:
                        pe.wait_ge(s_exp, n * (2 * NB) + first + t - 1)
                    if masked:
                        pe.matmul(e_ps[k % 2], ident_bf[:, :], neg_diag[:, :, :].rearrange("p l n -> p (l n)"),
                                  start=True, stop=False)
                    for r in range(L):
                        line = slice(r * S, (r + 1) * S)
                        last = pe.matmul(e_ps[k % 2][:, line], qk[k % 2][0:CQ, line], k_low[k % 2][:, line],
                                         start=not masked, stop=not masked or r == L - 1)
                    last.then_inc(s_e, 1)

                def rows_step(t, k):
                    if inside(k):
                        pe.wait_ge(s_xlo, n * NB + t + 1)
                        if k >= 2:
                            pe.wait_ge(s_qkev, n * NB + t - 1)
                        for c in range(CH):
                            for i, (w, m) in enumerate(((wqk_hi, xr_hi), (wqk_lo, xr_hi), (wqk_hi, xr_lo))):
                                last = pe.matmul(qk_ps[k % 2], w[:, c, :], m[k % 2][:, c, :],
                                                 start=c == 0 and i == 0, stop=c == CH - 1 and i == 2)
                        last.then_inc(s_qk, 1)
                    if inside(k - 1):
                        energies(t - 1, k - 1, 0, False)

                walk(pe, rows_step, 1)

                def cols_step(t, k):
                    energies(t, k, NB, True)

                walk(pe, cols_step, 0)

                pe.wait_ge(s_stat, (n + 1) * (2 * NB))
                pe.wait_ge(s_mkept, (n + 1) * (2 * NB))
                pe.transpose(stat_ps[:, 0:S], col_nmax[:, :], ident[0:S, 0:S])
                pe.transpose(stat_ps[:, S:2 * S], col_sum[:, :], ident[0:S, 0:S]).then_inc(s_statT, 1)
                pe.wait_ge(s_dve, n * CHAIN + COL_FACTOR_AT)
                pe.transpose(factor_ps, weight[:, 0, S:2 * S], ident[0:S, 0:S]).then_inc(s_fT, 1)

                def colw_step(t, k):
                    pe.wait_ge(s_cw, n * NB + t + 1)
                    if k >= 2:
                        pe.wait_ge(s_cwlo, n * NB + t - 1)
                    for r in range(L):
                        line = slice(r * S, (r + 1) * S)
                        last = pe.transpose(colw_ps[k % 2][:, line], weight[:, k % 2, line], ident[0:S, 0:S])
                    last.then_inc(s_cwT, 1)

                walk(pe, colw_step, 0)

                pe.wait_ge(s_cwlo, (n + 1) * NB)
                alone(pe)
                with pe.Fori(0, CH) as g:
                    pe.wait_ge(s_xclo, n * (CH * NP) + g * NP + NP)
                    pe.wait_ge(s_evA, SEED + n * (CH * NB // 2) + g * (NB // 2))
                    pe.wait_ge(s_evD, SEED + n * (CH * NB // 2) + g * (NB // 2))
                    for b in range(NB):
                        if b >= 4:
                            read = s_evA if b % 2 == 0 else s_evD
                            pe.wait_ge(read, SEED + n * (CH * NB // 2) + g * (NB // 2) + (b - 4) // 2 + 1)
                        for r in range(L):
                            col = b * L + r
                            for i, (w, m) in enumerate(((xc_hi, colw_hi), (xc_hi, colw_lo), (xc_lo, colw_hi))):
                                last = pe.matmul(col_ps[b % 4][:, r * S:(r + 1) * S], w[:, col, :], m[:, col, :],
                                                 start=i == 0, stop=i == 2)
                        last.then_inc(s_col, 1)

                def out_step(t, k):
                    if inside(k):
                        pe.wait_ge(s_rw, n * NB + t + 1)
                        if k >= 1:
                            pe.wait_ge(s_rwlo, n * NB + t)
                        for r in range(L):
                            line = slice(r * S, (r + 1) * S)
                            last = pe.transpose(roww_ps[:, line], weight[:, k % 2, line], ident[0:S, 0:S])
                        last.then_inc(s_rwT, 1)
                        x_loaded(pe, n, NB + CH * NP, t, k)
                    for r in range(4):
                        if inside(k):
                            if k >= 1 or r >= 2:
                                pe.wait_ge(s_xtlo, n * (L * NB) + t * L + r - 1)
                            for c in range(CH):
                                last = pe.transpose(xt_ps[r % 2][:, c * P:(c + 1) * P],
                                                    x_ring[:, k % XR, c * BL + r * S:c * BL + (r + 1) * S],
                                                    ident[:, :])
                            last.then_inc(s_xT, 1)
                        if inside(k - 1):
                            s = (k - 1) % 2
                            if r == 0:
                                pe.wait_ge(s_xtlo, n * (L * NB) + t * L)
                                pe.wait_ge(s_rwlo, n * NB + t)
                            if k - 1 >= 1 or r >= 2:
                                pe.wait_ge(s_av, n * (CH * NB) + (t - 1) * CH + r - 1)
                            for row in range(L):
                                line = slice(row * S, (row + 1) * S)
                                for i, (w, m) in enumerate(((xt_hi, roww_hi), (xt_hi, roww_lo), (xt_lo, roww_hi))):
                                    last = pe.matmul(row_ps[r % 2][:, line], w[s][:, row, r * P:(r + 1) * P],
                                                     m[s][:, line], start=i == 0, stop=i == 2)
                            last.then_inc(s_row, 1)
                        if inside(k - 2):
                            s = (k - 2) % 2
                            if k - 2 >= 1 or r >= 2:
                                pe.wait_ge(s_out, n * (CH * NB) + (t - 2) * CH + r - 1)
                            for c in range(CH):
                                if r == 0:
                                    pe.wait_ge(s_avlo, n * (CH * NB) + (t - 2) * CH + c + 1)
                                for i, (w, m) in enumerate(((wv_hi, av_hi), (wv_lo, av_hi), (wv_hi, av_lo))):
                                    last = pe.matmul(v_ps[r % 2], w[:, c, r * P:(r + 1) * P], m[s][:, c, :],
                                                     start=c == 0 and i == 0, stop=c == CH - 1 and i == 2)
                            last.then_inc(s_v, 1)

                walk(pe, out_step, 2)


def kernel(**inputs):
    import numpy as _np
    import concourse.bacc as _bacc
    from concourse import mybir as _mybir
    from concourse.bass_utils import run_bass_kernel_spmd as _run

    laid = {
        "x": _np.ascontiguousarray(inputs["x"]),
        "wqkT": _np.ascontiguousarray(_np.concatenate([inputs["L0_conv_wq"], inputs["L0_conv_wk"]], axis=0).T),
        "bqk": _np.concatenate([inputs["L0_conv_bq"], inputs["L0_conv_bk"]]).reshape(P, 1),
        "wvT": _np.ascontiguousarray(_np.asarray(inputs["L0_conv_wv"]).T),
        "bv": _np.ascontiguousarray(_np.asarray(inputs["L0_conv_bv"]).reshape(CH, P).T),
        "gamma": _np.ascontiguousarray(_np.broadcast_to(_np.asarray(inputs["L0_conv_gamma"]), (P, 1))),
    }
    nc = _bacc.Bacc("TRN2", target_bir_lowering=False, num_devices=1)
    arrays, args = {}, []
    for name, a in laid.items():
        arrays[f"in_{name}"] = a
        args.append(nc.dram_tensor(f"in_{name}", a.shape, _mybir.dt.from_np(a.dtype), kind="ExternalInput").ap())
    args.append(nc.dram_tensor("out_0", (N, C, H, W), _mybir.dt.float32, kind="ExternalOutput").ap())
    criss_cross(nc, *args)
    r = _run(nc, [arrays], core_ids=[0])
    return r.results[0]["out_0"]
```

```python
from contextlib import ExitStack

import concourse.bass as bass
from concourse import mybir

F32 = mybir.dt.float32
F32R = mybir.dt.float32r
F16 = mybir.dt.float16
BF16 = mybir.dt.bfloat16
U32 = mybir.dt.uint32
ALU = mybir.AluOpType
ACT = mybir.ActivationFunctionType
AX = mybir.AxisListType

P = 128
N, C, H, W = 8, 512, 96, 96
CQ = C // 8
S = 96
CH = C // P
L = 4
BL = L * S
NB = S // L
PX = H * W
XR = 4
CP = XR * 4
NP = P // CP
PS = NB // NP
KEPT = 2
POOL_CH = 2
SPILT = CH - KEPT
NEG = -1e30
P_SCALE = 4096.0
X_SCALE = 4096.0
TINY = 2.0 ** -100
EXPONENT = 0x7F800000


def walk(eng, step, tail, peel=XR):
    for t in range(peel):
        step(t, t)
    with eng.Fori(peel // XR, NB // XR) as j:
        for u in range(XR):
            step(j * XR + u, peel + u)
    for t in range(NB, NB + tail):
        step(t, t)


def loop(eng, step, unroll):
    with eng.Fori(0, NB // unroll) as j:
        for u in range(unroll):
            step(j * unroll + u, u, j)


def inside(k):
    return 0 <= k < NB


def criss_cross(nc, x, wqkT, bqk, wvT, bv, gamma, out):
    ctx = ExitStack()
    with ctx:
        def sb(name, shape, dt):
            return ctx.enter_context(nc.sbuf_tensor(name, shape, dt))

        def sem(name):
            return ctx.enter_context(nc.semaphore(name))

        row_exp_dram = nc.dram_tensor("row_exp_dram", (S, NB, BL), F32, kind="Internal").ap()
        spill_dram = nc.dram_tensor("spill_dram", (SPILT, P, PX), F32, kind="Internal").ap()

        x_rows = x.rearrange("n (c p) (b l) w -> n b p c (l w)", p=P, l=L)
        out_rows = out.rearrange("n (c p) (b l) w -> n b p c (l w)", p=P, l=L)
        x_cols = x.rearrange("n (g c) y w -> n g y c w", c=CP)

        wv_hi = sb("wv_hi", [P, CH, C], F32R)
        wv_lo = sb("wv_lo", [P, CH, C], F32R)
        wqk_hi = sb("wqk_hi", [P, CH, P], F32R)
        wqk_lo = sb("wqk_lo", [P, CH, P], F32R)
        ident = sb("ident", [P, P], F32)
        ident_bf = sb("ident_bf", [S, S], BF16)
        neg_diag = sb("neg_diag", [S, L, S], BF16)
        bqk_sb = sb("bqk_sb", [P, 1], F32)
        gamma_sb = sb("gamma_sb", [P, 1], F32)
        bv_sb = sb("bv_sb", [P, CH], F32)
        gbv = sb("gbv", [P, CH], F32)
        x_ring = sb("x_ring", [P, XR, CH * BL], F32)
        x_amax = sb("x_amax", [P, NB], F32)
        scale_sb = sb("scale_sb", [P, 8], F32)
        amax1, amax_all, x_scale, x_unscale, power = (scale_sb[:, i:i + 1] for i in range(5))
        neg_max = sb("neg_max", [S, 4, L], F32)
        exp_sum = sb("exp_sum", [S, 4, L], F32)
        nmax = sb("nmax", [S, 2 * S], F32)
        esum = sb("esum", [S, 2 * S], F32)
        row_nmax, col_nmax = nmax[:, 0:S], nmax[:, S:2 * S]
        row_sum, col_sum = esum[:, 0:S], esum[:, S:2 * S]
        row_factor = sb("row_factor", [S, S], F32)
        col_factor = sb("col_factor", [S, S], F32)
        weight = sb("weight", [S, 2, BL], F32)

        kept = sb("kept", [P, KEPT, PX], F32)
        qk_all = kept[:, 0, :]
        col_exp = kept[0:S, 1, :]
        LOWER = 2 * PX * 2 // 4
        UPPER = 2 * S * P * 2 // 4
        area = sb("area", [P, LOWER + UPPER], F32)

        AREA = nc.lookup_mloc(area).addr

        def part(at, name, shape, dt, parts=P):
            return nc.alloc_sbuf_tensor_at(name, [parts, *shape], dt, offset=AREA + 4 * at)

        HALF = CH * BL
        xr_hi = [part(i * HALF, f"xr_hi{i}", [CH, BL], F32R) for i in range(2)]
        xr_lo = [part((2 + i) * HALF, f"xr_lo{i}", [CH, BL], F32R) for i in range(2)]
        at = 4 * HALF
        row_exp = [part(at + i * BL, f"row_exp{i}", [L, S], F32, S) for i in range(4)]
        av = part(at, "av", [CH, BL], F32)
        at += 4 * BL
        qk = [part(at + i * BL, f"qk{i}", [BL], F32) for i in range(2)]
        k_low = [part(at + (2 + i) * BL, f"k_low{i}", [BL], F32, CQ) for i in range(2)]
        spill_in = [part(at + i * SPILT * BL, f"spill_in{i}", [SPILT, BL], F32) for i in range(2)]
        at += 4 * BL
        assert at <= LOWER and SPILT <= 2
        qk_col = [part(i * BL, f"qk_col{i}", [BL], F32) for i in range(4)]
        k_col = [part((4 + i) * BL, f"k_col{i}", [BL], F32, CQ) for i in range(4)]
        colw_hi = part(0, "colw_hi", [S, S], F16, S)
        colw_lo = part(PX // 2, "colw_lo", [S, S], F16, S)
        xc_hi = part(LOWER, "xc_hi", [S, P], F16, S)
        xc_lo = part(LOWER + UPPER // 2, "xc_lo", [S, P], F16, S)
        at = LOWER
        av_hi = [part(at + i * HALF, f"av_hi{i}", [CH, BL], F32R) for i in range(2)]
        at += 2 * HALF
        av_lo = [part(at + i * HALF, f"av_lo{i}", [CH, BL], F32R) for i in range(2)]
        at += 2 * HALF
        T16 = L * C // 2
        xt_hi = [part(at + i * T16, f"xt_hi{i}", [L, C], F16, S) for i in range(2)]
        at += 2 * T16
        xt_lo = [part(at + i * T16, f"xt_lo{i}", [L, C], F16, S) for i in range(2)]
        at += 2 * T16
        row_exp_in = [part(at + i * BL, f"row_exp_in{i}", [BL], F32, S) for i in range(2)]
        at += 2 * BL
        roww_hi = [part(at + i * BL // 2, f"roww_hi{i}", [BL], F16, S) for i in range(2)]
        at += BL
        roww_lo = [part(at + i * BL // 2, f"roww_lo{i}", [BL], F16, S) for i in range(2)]
        at += BL
        assert at <= LOWER + UPPER

        bank = [ctx.enter_context(nc.psum_tensor(f"bank{i}", [P, 512], F32)) for i in range(8)]
        qk_ps = [bank[0][:, 0:BL], bank[1][:, 0:BL]]
        e_ps = [bank[2 + i][0:S, 0:BL] for i in range(4)]
        stat_ps = bank[6][0:S, 0:2 * S]
        factor_ps = bank[7][0:S, 0:S]
        colw_ps = [bank[4][0:S, 0:BL], bank[5][0:S, 0:BL]]
        col_ps = [bank[i][:, 0:BL] for i in range(4)]
        xt_ps = [bank[4][0:S, :], bank[5][0:S, :]]
        roww_ps = bank[6][0:S, 0:BL]
        row_ps = [bank[0][:, 0:BL], bank[1][:, 0:BL]]
        v_ps = [bank[2][:, 0:BL], bank[3][:, 0:BL]]

        SEED = 1
        s_const = sem("const_loaded")
        s_gamma = sem("gamma_loaded")
        s_id0 = sem("ident_cleared")
        s_id = sem("ident_ready")
        s_gbv = sem("gamma_bv_ready")
        s_whi = sem("weights_hi_ready")
        s_wlo = sem("weights_lo_ready")
        s_xin = [sem(f"x_loaded{i}") for i in range(XR)]
        s_xhi = sem("xr_hi_ready")
        s_xlo = sem("xr_lo_first_ready")
        s_xlo2 = sem("xr_lo_second_ready")
        s_amax = sem("x_amax_ready")
        s_qk = sem("qk_projected")
        s_qkev = sem("qk_evacuated")
        s_big = sem("qk_kept")
        s_colqk = sem("qk_column_ready")
        s_klow = sem("k_low_ready")
        s_e = sem("energy_ready")
        s_nmax = sem("neg_max_ready")
        s_exp = sem("exp_ready")
        s_stat = sem("stats_kept")
        s_passed = sem("waits_passed")
        s_mkept = sem("neg_max_kept")
        s_rstore = [sem(f"row_exp_stored{i}") for i in range(XR)]
        s_sall = sem("amax_all_ready")
        s_statT = sem("col_stats_transposed")
        s_dve = sem("dve_chain")
        s_fexp = sem("factor_exp_ready")
        s_fT = sem("col_factor_transposed")
        s_colf = sem("col_factor_ready")
        s_cw = sem("col_weight_ready")
        s_cwT = sem("col_weight_transposed")
        s_cwhi = sem("colw_hi_ready")
        s_cwlo = sem("colw_lo_ready")
        s_xchi = sem("xc_hi_ready")
        s_xclo = sem("xc_lo_ready")
        s_col = sem("col_average_ready")
        s_evA = sem("col_average_even_kept")
        s_evD = sem("col_average_odd_kept")
        s_spill = [sem(f"col_average_spilt{g}") for g in range(SPILT)]
        s_spin = [sem(f"spill_loaded{i}") for i in range(2)]
        s_rin = [sem(f"row_exp_loaded{i}") for i in range(2)]
        s_rw = sem("row_weight_ready")
        s_rwT = sem("row_weight_transposed")
        s_rwhi = sem("roww_hi_ready")
        s_rwlo = sem("roww_lo_ready")
        s_xT = sem("x_transposed")
        s_xthi = sem("xt_hi_ready")
        s_xtlo = sem("xt_lo_ready")
        s_row = sem("row_average_ready")
        s_av = sem("average_ready")
        s_avhi = sem("av_hi_ready")
        s_avlo = sem("av_lo_ready")
        s_v = sem("value_ready")
        s_out = sem("output_ready")
        s_store = [sem(f"output_stored{i}") for i in range(XR)]

        AMAX_AT, SCALE_AT, MAX_AT, COL_FACTOR_AT, CHAIN = 1, 6, 10, 16, 17

        XPI = 2 * NB + CH * NP
        LPS = XPI // XR

        def x_loaded(eng, n, first, b, k):
            eng.wait_ge(s_xin[k % XR], 16 * (n * LPS + first // XR + (b - k % XR) // XR + 1)
                        if isinstance(b, int) else (n * LPS + first // XR + 1) * 16 + (b - k % XR) * (16 // XR))

        def slot_stored(eng, sems, n, b, k):
            eng.wait_ge(sems[k % XR], 16 * SEED + n * (16 * NB // XR) + (b - k % XR) * (16 // XR))

        def all_stored(eng, sems, n):
            for s in sems:
                eng.wait_ge(s, 16 * SEED + n * (16 * NB // XR))

        def alone(eng):
            eng.sem_inc(s_passed, 1)

        block = ctx.enter_context(nc.Block())

        @block.sync
        def _(sp):
            sp.dma_start(gamma_sb[:, :], gamma).then_inc(s_gamma, 16)
            sp.dma_start(x_ring[:, 0:2, :].rearrange("p s n -> p (s n)")[:, 0:CH * C].rearrange("p (c n) -> p c n", c=CH),
                         wvT.rearrange("(c p) n -> p c n", p=P)).then_inc(s_const, 16)
            sp.dma_start(x_ring[:, 2, 0:CH * P].rearrange("p (c n) -> p c n", c=CH),
                         wqkT.rearrange("(c p) n -> p c n", p=P)).then_inc(s_const, 16)
            sp.dma_start(bqk_sb[:, :], bqk).then_inc(s_const, 16)
            sp.dma_start(bv_sb[:, :], bv).then_inc(s_const, 16)
            for s in (*s_rstore, *s_store):
                sp.sem_inc(s, 16 * SEED)
            sp.wait_ge(s_wlo, 2)

            def load_rows(n, b, k):
                sp.dma_start(x_ring[:, k % XR, :].rearrange("p (c n) -> p c n", c=CH),
                             x_rows[n, b]).then_inc(s_xin[k % XR], 16)

            def load_cols(n, i, k):
                sp.dma_start(x_ring[0:S, k % XR, :].rearrange("p (c n) -> p c n", c=CP),
                             x_cols[n, i]).then_inc(s_xin[k % XR], 16)

            def image(n, more):
                def rows_step(t, k):
                    if XR <= k < NB + XR:
                        sp.wait_ge(s_xlo, n * NB + t - (XR - 1))
                        sp.wait_ge(s_xlo2, n * NB + t - (XR - 1))
                        sp.wait_ge(s_amax, n * NB + t - (XR - 1))
                        alone(sp)
                        if inside(k):
                            load_rows(n, t, k)
                        else:
                            load_cols(n, t - NB, k)
                    if inside(k - 8):
                        sp.wait_ge(s_exp, n * (2 * NB) + t - 7)
                        sp.dma_start(row_exp_dram[:, t - 8, :],
                                     row_exp[k % 4][:, :, :].rearrange("p l n -> p (l n)")).then_inc(s_rstore[k % 4], 16)

                walk(sp, rows_step, 8, 2 * XR)

                for g in range(CH):
                    for i in range(NP):
                        if g > 0 or i >= XR:
                            sp.wait_ge(s_xclo, n * (CH * NP) + g * NP + i - (XR - 1))
                            load_cols(n, g * NP + i, i)
                    if 1 <= g <= SPILT:
                        sp.wait_ge(s_evA, SEED + n * (CH * NB // 2) + g * (NB // 2))
                        sp.wait_ge(s_evD, SEED + n * (CH * NB // 2) + g * (NB // 2))
                        sp.dma_start(spill_dram[g - 1], kept[:, (g - 1) % KEPT, :]).then_inc(s_spill[g - 1], 16)

                def out_step(t, k):
                    if inside(k):
                        if k < XR:
                            sp.wait_ge(s_xclo, n * (CH * NP) + CH * NP - XR + 1 + k)
                        else:
                            slot_stored(sp, s_store, n, t, k)
                        load_rows(n, t, k)
                        if k == 0:
                            sp.wait_ge(s_col, SEED + (n + 1) * (CH * NB))
                            alone(sp)
                            for s in s_spill:
                                sp.wait_ge(s, n * 16 + 16)
                                alone(sp)
                            all_stored(sp, s_rstore, n + 1)
                        if k >= 2:
                            sp.wait_ge(s_rw, n * NB + t - 1)
                            alone(sp)
                        sp.dma_start(row_exp_in[k % 2][:, :], row_exp_dram[:, t, :]).then_inc(s_rin[k % 2], 16)
                        if k >= 2:
                            sp.wait_ge(s_av, n * (CH * NB) + t * CH - CH)
                        sp.dma_start(spill_in[k % 2][:, :, :], spill_dram.rearrange("c p (b n) -> b p c n", n=BL)[t])\
                            .then_inc(s_spin[k % 2], 16)
                    if inside(k - 3):
                        sp.wait_ge(s_out, n * (CH * NB) + t * CH - 2 * CH)
                        sp.dma_start(out_rows[n, t - 3],
                                     x_ring[:, (k - 3) % XR, :].rearrange("p (c n) -> p c n", c=CH))\
                            .then_inc(s_store[(k - 3) % XR], 16)
                    if k >= NB and more:
                        sp.wait_ge(s_store[k - NB], 16 * SEED + (n + 1) * (16 * NB // XR))
                        load_rows(n + 1, k - NB, k)

                walk(sp, out_step, 4)

            for b in range(XR):
                load_rows(0, b, b)
            with sp.Fori(0, N - 1) as n:
                image(n, True)
            image(N - 1, False)
            all_stored(sp, s_store, N)

        @block.gpsimd
        def _(pool):
            pool.memset(ident[:, :], 0.0).then_inc(s_id0, 1)
            pool.memset(ident_bf[:, :], 0.0).then_inc(s_id0, 1)
            pool.memset(neg_diag[:, :, :], 0.0).then_inc(s_id0, 1)
            pool.wait_ge(s_id0, 3)
            pool.affine_select(out=ident[:, :], in_=ident[:, :], compare_op=ALU.not_equal, fill=1.0, base=0,
                               pattern=[[-1, P]], channel_multiplier=1).then_inc(s_id, 1)
            pool.affine_select(out=ident_bf[:, :], in_=ident_bf[:, :], compare_op=ALU.not_equal, fill=1.0, base=0,
                               pattern=[[-1, S]], channel_multiplier=1).then_inc(s_id, 1)
            pool.affine_select(out=neg_diag[:, :, :], in_=neg_diag[:, :, :], compare_op=ALU.not_equal, fill=NEG,
                               base=0, pattern=[[0, L], [-1, S]], channel_multiplier=1).then_inc(s_id, 1)
            with pool.Fori(0, N) as n:
                def rows_step(t, k):
                    if inside(k):
                        x_loaded(pool, n, 0, t, k)
                        pool.wait_ge(s_xhi, n * NB + t + 1)
                        pool.tensor_tensor(xr_lo[k % 2][:, 0:POOL_CH, :].rearrange("p c n -> p (c n)"),
                                           x_ring[:, k % XR, 0:POOL_CH * BL],
                                           xr_hi[k % 2][:, 0:POOL_CH, :].rearrange("p c n -> p (c n)").bitcast(F32),
                                           ALU.subtract).then_inc(s_xlo, 1)
                    if inside(k - 2):
                        pool.wait_ge(s_qkev, n * NB + t - 1)
                        alone(pool)
                        pool.tensor_copy(qk_all[:, bass.ds((t - 2) * BL, BL)], qk[k % 2][:, :]).then_inc(s_big, 1)

                walk(pool, rows_step, 2)

                pool.wait_ge(s_dve, n * CHAIN + AMAX_AT)
                alone(pool)
                pool.partition_all_reduce(amax_all, amax1, P, bass.bass_isa.ReduceOp.max).then_inc(s_sall, 1)

                qk_by_col = qk_all.rearrange("p (y x) -> p x y", x=S)
                pool.wait_ge(s_big, (n + 1) * NB)
                alone(pool)

                def cols_step(t, k, j):
                    pool.wait_ge(s_e, n * (2 * NB) + NB + t - 3)
                    alone(pool)
                    pool.tensor_copy(qk_col[k % 4][:, :].rearrange("p (l y) -> p l y", l=L),
                                     qk_by_col[:, bass.ds(t * L, L), :]).then_inc(s_colqk, 1)

                loop(pool, cols_step, XR)

                pool.wait_ge(s_colf, n + 1)
                col_exp3 = col_exp.rearrange("p (x y) -> p x y", y=S)

                def colw_step(t, k):
                    if k >= 2:
                        pool.wait_ge(s_cwT, n * NB + t - 1)
                    pool.tensor_tensor(weight[:, k % 2, :].rearrange("p (l n) -> p l n", l=L),
                                       col_exp3[:, bass.ds(t * L, L), :],
                                       col_factor[:, bass.ds(t * L, L)].unsqueeze(2).to_broadcast([S, L, S]),
                                       ALU.mult).then_inc(s_cw, 1)

                walk(pool, colw_step, 0)

                pool.wait_ge(s_dve, (n + 1) * CHAIN)

                def out_step(t, k):
                    if inside(k):
                        pool.wait_ge(s_rin[k % 2], n * (8 * NB) + (t - k % 2) * 8 + 16)
                        if k >= 2:
                            pool.wait_ge(s_rwT, n * NB + t - 1)
                        else:
                            pool.wait_ge(s_cwT, (n + 1) * NB)
                        pool.tensor_tensor(weight[:, k % 2, :].rearrange("p (l n) -> p l n", l=L),
                                           row_exp_in[k % 2][:, :].rearrange("p (l n) -> p l n", l=L),
                                           row_factor[:, bass.ds(t * L, L)].unsqueeze(2).to_broadcast([S, L, S]),
                                           ALU.mult).then_inc(s_rw, 1)
                    if inside(k - 2):
                        for c in range(CH):
                            pool.wait_ge(s_avhi, n * (CH * NB) + (t - 2) * CH + c + 1)
                            pool.tensor_tensor(av_lo[k % 2][:, c, :], av[:, c, :],
                                               av_hi[k % 2][:, c, :].bitcast(F32), ALU.subtract).then_inc(s_avlo, 1)

                walk(pool, out_step, 2)

        @block.scalar
        def _(act):
            act.wait_ge(s_gamma, 16)
            act.wait_ge(s_const, 64)
            wv_in = x_ring[:, 0:2, :].rearrange("p s n -> p (s n)")[:, 0:CH * C].rearrange("p (c n) -> p c n", c=CH)
            wqk_in = x_ring[:, 2, 0:CH * P].rearrange("p (c n) -> p c n", c=CH)
            act.activation(wv_hi[:, :, :], wv_in, ACT.Copy, scale=gamma_sb[:, 0:1]).then_inc(s_whi, 1)
            act.activation(wqk_hi[:, :, :], wqk_in, ACT.Copy).then_inc(s_whi, 1)
            with act.Fori(0, N) as n:
                def exps(t, k, first, dest):
                    act.wait_ge(s_nmax, n * (2 * NB) + first + t + 1)
                    for r in range(L):
                        last = act.activation(dest[:, r, :], e_ps[k % 4][:, r * S:(r + 1) * S], ACT.Exp,
                                              bias=neg_max[:, k % 4, r:r + 1], accum_out=exp_sum[:, k % 4, r:r + 1])
                    last.then_inc(s_exp, 1)

                def rows_step(t, k):
                    if inside(k):
                        x_loaded(act, n, 0, t, k)
                        if k >= 2:
                            act.wait_ge(s_qk, n * NB + t - 1)
                        act.activation(xr_hi[k % 2][:, :, :].rearrange("p c n -> p (c n)"), x_ring[:, k % XR, :],
                                       ACT.Copy).then_inc(s_xhi, 1)
                    if inside(k - 2):
                        act.wait_ge(s_qk, n * NB + t - 1)
                        if k - 2 >= 2:
                            act.wait_ge(s_big, n * NB + t - 3)
                            act.wait_ge(s_e, n * (2 * NB) + t - 3)
                        act.activation(qk[k % 2][:, :], qk_ps[k % 2], ACT.Identity,
                                       bias=bqk_sb[:, 0:1]).then_inc(s_qkev, 1)
                    if inside(k - 5):
                        if k - 5 >= 4:
                            slot_stored(act, s_rstore, n, t - 5, k - 5)
                            act.wait_ge(s_stat, n * (2 * NB) + t - 8)
                        exps(t - 5, k - 5, 0, row_exp[(k - 5) % 4][:, :, :])

                walk(act, rows_step, 5, 3 * XR)

                col_exp3 = col_exp.rearrange("p (x y) -> p x y", y=S)

                def split_piece(g, i, k):
                    x_loaded(act, n, NB + g * NP, i, k)
                    act.activation(xc_hi[:, :, bass.ds(i * CP, CP)].rearrange("p x c -> p c x"),
                                   x_ring[0:S, k % XR, :].rearrange("p (c n) -> p c n", c=CP), ACT.Copy,
                                   scale=x_scale[0:S, :]).then_inc(s_xchi, 1)

                act.wait_ge(s_dve, n * CHAIN + SCALE_AT)

                def cols_step(t, k, j):
                    if k % PS == 0:
                        split_piece(0, j * XR + k // PS, k // PS)
                    act.wait_ge(s_stat, n * (2 * NB) + NB + t - 3)
                    exps(t, k, NB, col_exp3[:, bass.ds(t * L, L), :])

                loop(act, cols_step, PS * XR)

                act.wait_ge(s_dve, n * CHAIN + MAX_AT)
                act.activation(row_nmax, row_nmax, ACT.Exp).then_inc(s_fexp, 1)
                act.activation(row_factor[:, :], row_factor[:, :], ACT.Exp).then_inc(s_fexp, 1)

                all_stored(act, s_rstore, n + 1)

                def colw_step(t, k):
                    act.wait_ge(s_cwT, n * NB + t + 1)
                    act.activation(colw_hi[:, bass.ds(t * L, L), :],
                                   colw_ps[k % 2].rearrange("p (l n) -> p l n", l=L), ACT.Copy).then_inc(s_cwhi, 1)

                walk(act, colw_step, 0)

                for g in range(CH):
                    if g >= KEPT:
                        act.wait_ge(s_spill[g - KEPT], n * 16 + 16)
                    kept_by_col = kept[:, g % KEPT, :].rearrange("p (y x) -> p x y", x=S)
                    with act.Fori(0, NB // 4) as j:
                        for u in (0, 2):
                            act.wait_ge(s_col, SEED + n * (CH * NB) + g * NB + j * 4 + u + 1)
                            act.activation(kept_by_col[:, bass.ds(j * (4 * L) + u * L, L), :],
                                           col_ps[u].rearrange("p (l n) -> p l n", l=L), ACT.Copy,
                                           scale=x_unscale).then_inc(s_evA, 1)
                    if g < CH - 1:
                        act.wait_ge(s_col, SEED + n * (CH * NB) + (g + 1) * NB)
                        for i in range(NP):
                            split_piece(g + 1, i, i)

                def out_step(t, k):
                    if inside(k):
                        act.wait_ge(s_rwT, n * NB + t + 1)
                        if k >= 2:
                            act.wait_ge(s_row, n * (CH * NB) + t * CH - CH)
                        elif k == 0:
                            act.wait_ge(s_col, SEED + (n + 1) * (CH * NB))
                        act.activation(roww_hi[k % 2][:, :], roww_ps, ACT.Copy).then_inc(s_rwhi, 1)
                    for r in range(4):
                        if inside(k):
                            act.wait_ge(s_xT, n * (L * NB) + t * L + r + 1)
                            act.activation(xt_hi[k % 2][:, r, :], xt_ps[r % 2], ACT.Copy,
                                           scale=x_scale[0:S, :]).then_inc(s_xthi, 1)
                        if inside(k - 1):
                            act.wait_ge(s_av, n * (CH * NB) + (t - 1) * CH + r + 1)
                            if k - 1 >= 2 and r == 0:
                                act.wait_ge(s_v, SEED + n * (CH * NB) + (t - 2) * CH)
                            act.activation(av_hi[(k - 1) % 2][:, r, :], av[:, r, :], ACT.Copy).then_inc(s_avhi, 1)

                walk(act, out_step, 1)

        @block.vector
        def _(dve):
            wv_in = x_ring[:, 0:2, :].rearrange("p s n -> p (s n)")[:, 0:CH * C].rearrange("p (c n) -> p c n", c=CH)
            wqk_in = x_ring[:, 2, 0:CH * P].rearrange("p (c n) -> p c n", c=CH)
            dve.wait_ge(s_const, 64)
            dve.wait_ge(s_gamma, 16)
            dve.tensor_scalar(gbv[:, :], bv_sb[:, :], gamma_sb[:, 0:1], None, ALU.mult).then_inc(s_gbv, 1)
            dve.wait_ge(s_gbv, 1)
            dve.wait_ge(s_whi, 2)
            dve.scalar_tensor_tensor(out=wv_lo[:, :, :], in0=wv_in, scalar=gamma_sb[:, 0:1],
                                     in1=wv_hi[:, :, :].bitcast(F32), op0=ALU.mult,
                                     op1=ALU.subtract).then_inc(s_wlo, 1)
            dve.tensor_tensor(wqk_lo[:, :, :], wqk_in, wqk_hi[:, :, :].bitcast(F32), ALU.subtract).then_inc(s_wlo, 1)
            with dve.Fori(0, N) as n:
                def line_max(b, k):
                    dve.wait_ge(s_e, n * (2 * NB) + b + 1)
                    if k >= 4:
                        dve.wait_ge(s_exp, n * (2 * NB) + b - 3)
                    dve.tensor_reduce(neg_max[:, k % 4, :], e_ps[k % 4].rearrange("p (l n) -> p l n", l=L), AX.X,
                                      ALU.max, negate=True).then_inc(s_nmax, 1)
                    dve.wait_ge(s_nmax, n * (2 * NB) + b + 1)
                    dve.tensor_copy(nmax[:, bass.ds(b * L, L)], neg_max[:, k % 4, :]).then_inc(s_mkept, 1)

                def line_sum(b, k):
                    dve.wait_ge(s_exp, n * (2 * NB) + b + 1)
                    dve.tensor_copy(esum[:, bass.ds(b * L, L)], exp_sum[:, k % 4, :]).then_inc(s_stat, 1)

                def rows_step(t, k):
                    if inside(k):
                        x_loaded(dve, n, 0, t, k)
                        dve.wait_ge(s_xhi, n * NB + t + 1)
                        dve.tensor_tensor(xr_lo[k % 2][:, POOL_CH:CH, :].rearrange("p c n -> p (c n)"),
                                          x_ring[:, k % XR, POOL_CH * BL:CH * BL],
                                          xr_hi[k % 2][:, POOL_CH:CH, :].rearrange("p c n -> p (c n)").bitcast(F32),
                                          ALU.subtract).then_inc(s_xlo2, 1)
                        dve.tensor_reduce(x_amax[:, bass.ds(t, 1)], x_ring[:, k % XR, :], AX.X, ALU.max,
                                          apply_absolute_value=True).then_inc(s_amax, 1)
                    if inside(k - 2):
                        dve.wait_ge(s_qkev, n * NB + t - 1)
                        if k - 2 >= 2:
                            dve.wait_ge(s_e, n * (2 * NB) + t - 3)
                        dve.tensor_copy(k_low[k % 2][:, :], qk[k % 2][CQ:2 * CQ, :]).then_inc(s_klow, 1)
                    if inside(k - 4):
                        line_max(t - 4, k - 4)
                    if inside(k - 6):
                        line_sum(t - 6, k - 6)

                walk(dve, rows_step, 2, 3 * XR)

                done = [0]

                def chain(ins):
                    done[0] += 1
                    ins.then_inc(s_dve, 1)
                    dve.wait_ge(s_dve, n * CHAIN + done[0])

                dve.wait_ge(s_amax, (n + 1) * NB)
                chain(dve.tensor_reduce(amax1, x_amax[:, :], AX.X, ALU.max))
                assert done[0] == AMAX_AT
                dve.wait_ge(s_sall, n + 1)
                chain(dve.tensor_scalar(amax_all, amax_all, TINY, None, ALU.max))
                chain(dve.tensor_scalar(power.bitcast(U32), amax_all.bitcast(U32), EXPONENT, None, ALU.bitwise_and))
                chain(dve.tensor_scalar(x_scale.bitcast(U32), amax_all.bitcast(U32), EXPONENT, EXPONENT,
                                        ALU.bitwise_xor, ALU.bitwise_and))
                chain(dve.tensor_scalar(x_unscale, power, 0.5 / (X_SCALE * P_SCALE), None, ALU.mult))
                chain(dve.tensor_scalar(x_scale, x_scale, X_SCALE, None, ALU.mult))
                assert done[0] == SCALE_AT

                def split_piece(g, i, k):
                    dve.wait_ge(s_xchi, n * (CH * NP) + g * NP + i + 1)
                    cols = xc_lo[:, :, bass.ds(i * CP, CP)], xc_hi[:, :, bass.ds(i * CP, CP)]
                    lo, hi = (v.rearrange("p x c -> p c x") for v in cols)
                    dve.scalar_tensor_tensor(out=lo, in0=x_ring[0:S, k % XR, :].rearrange("p (c n) -> p c n", c=CP),
                                             scalar=x_scale[0:S, :], in1=hi, op0=ALU.mult,
                                             op1=ALU.subtract).then_inc(s_xclo, 1)

                def cols_step(t, k, j):
                    dve.wait_ge(s_colqk, n * NB + t + 1)
                    dve.wait_ge(s_e, n * (2 * NB) + NB + t - 3)
                    dve.tensor_copy(k_col[k % 4][:, :], qk_col[k % 4][CQ:2 * CQ, :]).then_inc(s_klow, 1)
                    line_max(NB + t - 2, 4 + k - 2 + 4)
                    line_sum(NB + t - 4, 4 + k - 4 + 4)
                    if k % PS == PS - 1:
                        split_piece(0, j * XR + k // PS, k // PS)

                alone(dve)
                loop(dve, cols_step, PS * XR)
                line_max(2 * NB - 2, 2 * NB - 2)
                line_sum(2 * NB - 4, 2 * NB - 4)
                line_max(2 * NB - 1, 2 * NB - 1)
                for b in range(2 * NB - 3, 2 * NB):
                    line_sum(b, b)

                dve.wait_ge(s_mkept, (n + 1) * (2 * NB))
                dve.wait_ge(s_stat, (n + 1) * (2 * NB))
                dve.wait_ge(s_statT, n + 1)
                joint = weight[:, 0, 0:S]
                col_sumT = weight[:, 0, S:2 * S]
                chain(dve.tensor_tensor(joint, stat_ps[:, 0:S], row_nmax, ALU.min))
                chain(dve.tensor_copy(col_sumT, stat_ps[:, S:2 * S]))
                chain(dve.tensor_tensor(row_nmax, joint, row_nmax, ALU.subtract))
                chain(dve.tensor_tensor(row_factor[:, :], joint, stat_ps[:, 0:S], ALU.subtract))
                assert done[0] == MAX_AT
                dve.wait_ge(s_fexp, 2 * n + 2)
                chain(dve.tensor_tensor(row_sum, row_sum, row_nmax, ALU.mult))
                chain(dve.tensor_tensor(col_sumT, col_sumT, row_factor[:, :], ALU.mult))
                chain(dve.tensor_tensor(joint, row_sum, col_sumT, ALU.add))
                chain(dve.reciprocal(joint, joint))
                chain(dve.tensor_scalar(joint, joint, P_SCALE, None, ALU.mult))
                chain(dve.tensor_tensor(col_sumT, row_factor[:, :], joint, ALU.mult))
                assert done[0] == COL_FACTOR_AT
                chain(dve.tensor_tensor(row_factor[:, :], row_nmax, joint, ALU.mult))
                assert done[0] == CHAIN
                dve.wait_ge(s_fT, n + 1)
                dve.tensor_copy(col_factor[:, :], factor_ps).then_inc(s_colf, 1)

                def colw_step(t, k):
                    dve.wait_ge(s_cwhi, n * NB + t + 1)
                    dve.tensor_tensor(colw_lo[:, bass.ds(t * L, L), :],
                                      colw_ps[k % 2].rearrange("p (l n) -> p l n", l=L),
                                      colw_hi[:, bass.ds(t * L, L), :], ALU.subtract).then_inc(s_cwlo, 1)

                walk(dve, colw_step, 0)

                for g in range(CH):
                    if g >= KEPT:
                        dve.wait_ge(s_spill[g - KEPT], n * 16 + 16)
                        alone(dve)
                    kept_by_col = kept[:, g % KEPT, :].rearrange("p (y x) -> p x y", x=S)
                    with dve.Fori(0, NB // 4) as j:
                        for u in (1, 3):
                            dve.wait_ge(s_col, SEED + n * (CH * NB) + g * NB + j * 4 + u + 1)
                            dve.tensor_scalar(kept_by_col[:, bass.ds(j * (4 * L) + u * L, L), :],
                                              col_ps[u].rearrange("p (l n) -> p l n", l=L), x_unscale, None,
                                              ALU.mult).then_inc(s_evD, 1)
                    if g < CH - 1:
                        for i in range(NP):
                            split_piece(g + 1, i, i)

                dve.wait_ge(s_evA, SEED + (n + 1) * (CH * NB // 2))

                def out_step(t, k):
                    if inside(k):
                        dve.wait_ge(s_rwhi, n * NB + t + 1)
                        dve.tensor_tensor(roww_lo[k % 2][:, :], roww_ps, roww_hi[k % 2][:, :], ALU.subtract).then_inc(s_rwlo, 1)
                    for r in range(4):
                        if inside(k):
                            dve.wait_ge(s_xthi, n * (L * NB) + t * L + r + 1)
                            dve.scalar_tensor_tensor(out=xt_lo[k % 2][:, r, :], in0=xt_ps[r % 2],
                                                     scalar=x_scale[0:S, :], in1=xt_hi[k % 2][:, r, :],
                                                     op0=ALU.mult, op1=ALU.subtract).then_inc(s_xtlo, 1)
                        if inside(k - 1):
                            dve.wait_ge(s_row, n * (CH * NB) + (t - 1) * CH + r + 1)
                            if k - 1 >= 1:
                                dve.wait_ge(s_avlo, n * (CH * NB) + (t - 2) * CH + r + 1)
                            if r < SPILT:
                                if r == 0:
                                    dve.wait_ge(s_spin[(k - 1) % 2], n * (8 * NB) + (t - 1 - (k - 1) % 2) * 8 + 16)
                                col = spill_in[(k - 1) % 2][:, r, :]
                            else:
                                col = kept[:, r % KEPT, bass.ds((t - 1) * BL, BL)]
                            dve.scalar_tensor_tensor(out=av[:, r, :], in0=row_ps[r % 2], scalar=x_unscale, in1=col,
                                                     op0=ALU.mult, op1=ALU.add).then_inc(s_av, 1)
                        if inside(k - 2):
                            dve.wait_ge(s_v, SEED + n * (CH * NB) + (t - 2) * CH + r + 1)
                            res = x_ring[:, (k - 2) % XR, r * BL:(r + 1) * BL]
                            dve.scalar_tensor_tensor(out=res, in0=v_ps[r % 2], scalar=gbv[:, r:r + 1], in1=res,
                                                     op0=ALU.add, op1=ALU.add).then_inc(s_out, 1)

                walk(dve, out_step, 2)

        @block.tensor
        def _(pe):
            for s in (s_v, s_col, s_evA, s_evD):
                pe.sem_inc(s, SEED)
            pe.wait_ge(s_id, 3)
            pe.wait_ge(s_wlo, 2)
            with pe.Fori(0, N) as n:
                def energies(t, k, first, masked, q, kk):
                    pe.wait_ge(s_klow, n * (2 * NB) + first + t + 1)
                    if k >= 4 or first:
                        pe.wait_ge(s_exp, n * (2 * NB) + first + t - 3)
                    if masked:
                        pe.matmul(e_ps[k % 4], ident_bf[:, :], neg_diag[:, :, :].rearrange("p l n -> p (l n)"),
                                  start=True, stop=False)
                    for r in range(L):
                        line = slice(r * S, (r + 1) * S)
                        last = pe.matmul(e_ps[k % 4][:, line], q[0:CQ, line], kk[:, line],
                                         start=not masked, stop=not masked or r == L - 1)
                    last.then_inc(s_e, 1)

                def rows_step(t, k):
                    if inside(k):
                        pe.wait_ge(s_xlo, n * NB + t + 1)
                        pe.wait_ge(s_xlo2, n * NB + t + 1)
                        if k >= 2:
                            pe.wait_ge(s_qkev, n * NB + t - 1)
                        for c in range(CH):
                            for i, (w, m) in enumerate(((wqk_hi, xr_hi), (wqk_lo, xr_hi), (wqk_hi, xr_lo))):
                                last = pe.matmul(qk_ps[k % 2], w[:, c, :], m[k % 2][:, c, :],
                                                 start=c == 0 and i == 0, stop=c == CH - 1 and i == 2)
                        last.then_inc(s_qk, 1)
                    if inside(k - 2):
                        energies(t - 2, k - 2, 0, False, qk[k % 2], k_low[k % 2])

                walk(pe, rows_step, 2)

                def cols_step(t, k, j):
                    energies(t, k, NB, True, qk_col[k % 4], k_col[k % 4])

                loop(pe, cols_step, XR)

                pe.wait_ge(s_stat, (n + 1) * (2 * NB))
                pe.wait_ge(s_mkept, (n + 1) * (2 * NB))
                pe.transpose(stat_ps[:, 0:S], col_nmax, ident[0:S, 0:S])
                pe.transpose(stat_ps[:, S:2 * S], col_sum, ident[0:S, 0:S]).then_inc(s_statT, 1)
                pe.wait_ge(s_dve, n * CHAIN + COL_FACTOR_AT)
                pe.transpose(factor_ps, weight[:, 0, S:2 * S], ident[0:S, 0:S]).then_inc(s_fT, 1)

                def colw_step(t, k):
                    pe.wait_ge(s_cw, n * NB + t + 1)
                    if k >= 2:
                        pe.wait_ge(s_cwlo, n * NB + t - 1)
                    for r in range(L):
                        line = slice(r * S, (r + 1) * S)
                        last = pe.transpose(colw_ps[k % 2][:, line], weight[:, k % 2, line], ident[0:S, 0:S])
                    last.then_inc(s_cwT, 1)

                walk(pe, colw_step, 0)

                pe.wait_ge(s_cwlo, (n + 1) * NB)
                alone(pe)
                with pe.Fori(0, CH) as g:
                    pe.wait_ge(s_xclo, n * (CH * NP) + g * NP + NP)
                    pe.wait_ge(s_evA, SEED + n * (CH * NB // 2) + g * (NB // 2))
                    pe.wait_ge(s_evD, SEED + n * (CH * NB // 2) + g * (NB // 2))
                    for b in range(NB):
                        if b >= 4:
                            read = s_evA if b % 2 == 0 else s_evD
                            pe.wait_ge(read, SEED + n * (CH * NB // 2) + g * (NB // 2) + (b - 4) // 2 + 1)
                        for r in range(L):
                            col = b * L + r
                            for i, (w, m) in enumerate(((xc_hi, colw_hi), (xc_hi, colw_lo), (xc_lo, colw_hi))):
                                last = pe.matmul(col_ps[b % 4][:, r * S:(r + 1) * S], w[:, col, :], m[:, col, :],
                                                 start=i == 0, stop=i == 2)
                        last.then_inc(s_col, 1)

                def out_step(t, k):
                    if inside(k):
                        pe.wait_ge(s_rw, n * NB + t + 1)
                        if k >= 1:
                            pe.wait_ge(s_rwlo, n * NB + t)
                        for r in range(L):
                            line = slice(r * S, (r + 1) * S)
                            last = pe.transpose(roww_ps[:, line], weight[:, k % 2, line], ident[0:S, 0:S])
                        last.then_inc(s_rwT, 1)
                        x_loaded(pe, n, NB + CH * NP, t, k)
                    for r in range(4):
                        if inside(k):
                            if k >= 1 or r >= 2:
                                pe.wait_ge(s_xtlo, n * (L * NB) + t * L + r - 1)
                            for c in range(CH):
                                last = pe.transpose(xt_ps[r % 2][:, c * P:(c + 1) * P],
                                                    x_ring[:, k % XR, c * BL + r * S:c * BL + (r + 1) * S],
                                                    ident[:, :])
                            last.then_inc(s_xT, 1)
                        if inside(k - 1):
                            s = (k - 1) % 2
                            if r == 0:
                                pe.wait_ge(s_xtlo, n * (L * NB) + t * L)
                                pe.wait_ge(s_rwlo, n * NB + t)
                            if k - 1 >= 1 or r >= 2:
                                pe.wait_ge(s_av, n * (CH * NB) + (t - 1) * CH + r - 1)
                            for row in range(L):
                                line = slice(row * S, (row + 1) * S)
                                for i, (w, m) in enumerate(((xt_hi, roww_hi), (xt_hi, roww_lo), (xt_lo, roww_hi))):
                                    last = pe.matmul(row_ps[r % 2][:, line], w[s][:, row, r * P:(r + 1) * P],
                                                     m[s][:, line], start=i == 0, stop=i == 2)
                            last.then_inc(s_row, 1)
                        if inside(k - 2):
                            s = (k - 2) % 2
                            if k - 2 >= 1 or r >= 2:
                                pe.wait_ge(s_out, n * (CH * NB) + (t - 2) * CH + r - 1)
                            for c in range(CH):
                                if r == 0:
                                    pe.wait_ge(s_avlo, n * (CH * NB) + (t - 2) * CH + c + 1)
                                for i, (w, m) in enumerate(((wv_hi, av_hi), (wv_lo, av_hi), (wv_hi, av_lo))):
                                    last = pe.matmul(v_ps[r % 2], w[:, c, r * P:(r + 1) * P], m[s][:, c, :],
                                                     start=c == 0 and i == 0, stop=c == CH - 1 and i == 2)
                            last.then_inc(s_v, 1)

                walk(pe, out_step, 2)


def kernel(**inputs):
    import numpy as _np
    import concourse.bacc as _bacc
    from concourse import mybir as _mybir
    from concourse.bass_utils import run_bass_kernel_spmd as _run

    laid = {
        "x": _np.ascontiguousarray(inputs["x"]),
        "wqkT": _np.ascontiguousarray(_np.concatenate([inputs["L0_conv_wq"], inputs["L0_conv_wk"]], axis=0).T),
        "bqk": _np.concatenate([inputs["L0_conv_bq"], inputs["L0_conv_bk"]]).reshape(P, 1),
        "wvT": _np.ascontiguousarray(_np.asarray(inputs["L0_conv_wv"]).T),
        "bv": _np.ascontiguousarray(_np.asarray(inputs["L0_conv_bv"]).reshape(CH, P).T),
        "gamma": _np.ascontiguousarray(_np.broadcast_to(_np.asarray(inputs["L0_conv_gamma"]), (P, 1))),
    }
    nc = _bacc.Bacc("TRN2", target_bir_lowering=False, num_devices=1)
    arrays, args = {}, []
    for name, a in laid.items():
        arrays[f"in_{name}"] = a
        args.append(nc.dram_tensor(f"in_{name}", a.shape, _mybir.dt.from_np(a.dtype), kind="ExternalInput").ap())
    args.append(nc.dram_tensor("out_0", (N, C, H, W), _mybir.dt.float32, kind="ExternalOutput").ap())
    criss_cross(nc, *args)
    r = _run(nc, [arrays], core_ids=[0])
    return r.results[0]["out_0"]
```

```python
from contextlib import ExitStack

import concourse.bass as bass
from concourse import mybir

F32 = mybir.dt.float32
F32R = mybir.dt.float32r
F16 = mybir.dt.float16
BF16 = mybir.dt.bfloat16
U32 = mybir.dt.uint32
ALU = mybir.AluOpType
ACT = mybir.ActivationFunctionType
AX = mybir.AxisListType

P = 128
N, C, H, W = 8, 512, 96, 96
CQ = C // 8
S = 96
CH = C // P
L = 4
BL = L * S
NB = S // L
PX = H * W
XR = 4
CP = XR * 4
NP = P // CP
PS = NB // NP
KEPT = 2
POOL_CH = 3
SPILT = CH - KEPT
NEG = -1e30
P_SCALE = 4096.0
X_SCALE = 4096.0
TINY = 2.0 ** -100
EXPONENT = 0x7F800000


def walk(eng, step, tail, peel=XR):
    for t in range(peel):
        step(t, t)
    with eng.Fori(peel // XR, NB // XR) as j:
        for u in range(XR):
            step(j * XR + u, peel + u)
    for t in range(NB, NB + tail):
        step(t, t)


def loop(eng, step, unroll):
    with eng.Fori(0, NB // unroll) as j:
        for u in range(unroll):
            step(j * unroll + u, u, j)


def inside(k):
    return 0 <= k < NB


def criss_cross(nc, x, wqkT, bqk, wvT, bv, gamma, out):
    ctx = ExitStack()
    with ctx:
        def sb(name, shape, dt):
            return ctx.enter_context(nc.sbuf_tensor(name, shape, dt))

        def sem(name):
            return ctx.enter_context(nc.semaphore(name))

        row_exp_dram = nc.dram_tensor("row_exp_dram", (S, NB, BL), F32, kind="Internal").ap()
        spill_dram = nc.dram_tensor("spill_dram", (SPILT, P, PX), F32, kind="Internal").ap()

        x_rows = x.rearrange("n (c p) (b l) w -> n b p c (l w)", p=P, l=L)
        out_rows = out.rearrange("n (c p) (b l) w -> n b p c (l w)", p=P, l=L)
        x_cols = x.rearrange("n (g c) y w -> n g y c w", c=CP)

        wv_hi = sb("wv_hi", [P, CH, C], F32R)
        wv_lo = sb("wv_lo", [P, CH, C], F32R)
        wqk_hi = sb("wqk_hi", [P, CH, P], F32R)
        wqk_lo = sb("wqk_lo", [P, CH, P], F32R)
        ident = sb("ident", [P, P], F32)
        ident_bf = sb("ident_bf", [S, S], BF16)
        neg_diag = sb("neg_diag", [S, L, S], BF16)
        bqk_sb = sb("bqk_sb", [P, 1], F32)
        gamma_sb = sb("gamma_sb", [P, 1], F32)
        bv_sb = sb("bv_sb", [P, CH], F32)
        gbv = sb("gbv", [P, CH], F32)
        x_ring = sb("x_ring", [P, XR, CH * BL], F32)
        x_amax = sb("x_amax", [P, NB], F32)
        scale_sb = sb("scale_sb", [P, 8], F32)
        amax1, amax_all, x_scale, x_unscale, power = (scale_sb[:, i:i + 1] for i in range(5))
        block_stats = sb("block_stats", [S, 4, 2, L], F32)
        neg_max, exp_sum = block_stats[:, :, 0, :], block_stats[:, :, 1, :]
        stats = sb("stats", [S, 2, 2 * S], F32)
        row_nmax, col_nmax = stats[:, 0, 0:S], stats[:, 0, S:2 * S]
        row_sum, col_sum = stats[:, 1, 0:S], stats[:, 1, S:2 * S]
        row_factor = sb("row_factor", [S, S], F32)
        col_factor = sb("col_factor", [S, S], F32)
        weight = sb("weight", [S, 2, BL], F32)

        kept = sb("kept", [P, KEPT, PX], F32)
        qk_all = kept[:, 0, :]
        early = kept[0:S, :, 0:(NP - XR) * CP * S].rearrange("p k (i c n) -> p k i c n", i=NP - XR, c=CP)
        col_exp = kept[0:S, 1, :]
        LOWER = 2 * PX * 2 // 4
        UPPER = 2 * S * P * 2 // 4
        area = sb("area", [P, LOWER + UPPER], F32)

        AREA = nc.lookup_mloc(area).addr

        def part(at, name, shape, dt, parts=P):
            return nc.alloc_sbuf_tensor_at(name, [parts, *shape], dt, offset=AREA + 4 * at)

        HALF = CH * BL
        HALVES_AT = (0, 1, LOWER // HALF + 4, LOWER // HALF + 5)
        assert LOWER % HALF == 0 and UPPER == 8 * HALF
        xr_hi = [part(at * HALF, f"xr_hi{i}", [CH, BL], F32R) for i, at in enumerate(HALVES_AT)]
        xr_lo = [part((at + 2) * HALF, f"xr_lo{i}", [CH, BL], F32R) for i, at in enumerate(HALVES_AT)]
        at = 4 * HALF
        row_exp = [part(at + i * BL, f"row_exp{i}", [L, S], F32, S) for i in range(4)]
        av = part(at, "av", [CH, BL], F32)
        at += 4 * BL
        q_low = [part(at + i * BL, f"q_low{i}", [BL], F32, CQ) for i in range(2)]
        k_low = [part(at + (2 + i) * BL, f"k_low{i}", [BL], F32, CQ) for i in range(2)]
        spill_in = [part(at + i * SPILT * BL, f"spill_in{i}", [SPILT, BL], F32) for i in range(2)]
        at += 4 * BL
        assert at <= LOWER and SPILT <= 2
        qk_col = [part(i * BL, f"qk_col{i}", [BL], F32) for i in range(4)]
        k_col = [part((4 + i) * BL, f"k_col{i}", [BL], F32, CQ) for i in range(4)]
        COLW_AT = (NP - XR) * CP * S
        col_weight = kept[0:S, 0, COLW_AT:COLW_AT + 4 * BL].rearrange("p (i n) -> p i n", i=4)
        colw_hi = part(0, "colw_hi", [S, S], F16, S)
        colw_lo = part(PX // 2, "colw_lo", [S, S], F16, S)
        xc_hi = part(LOWER, "xc_hi", [S, P], F16, S)
        xc_lo = part(LOWER + UPPER // 2, "xc_lo", [S, P], F16, S)
        at = LOWER
        av_hi = [part(at + i * HALF, f"av_hi{i}", [CH, BL], F32R) for i in range(2)]
        at += 2 * HALF
        av_lo = [part(at + i * HALF, f"av_lo{i}", [CH, BL], F32R) for i in range(2)]
        at += 2 * HALF
        T16 = L * C // 2
        xt_hi = [part(at + i * T16, f"xt_hi{i}", [L, C], F16, S) for i in range(2)]
        at += 2 * T16
        xt_lo = [part(at + i * T16, f"xt_lo{i}", [L, C], F16, S) for i in range(2)]
        at += 2 * T16
        row_exp_in = [part(at + i * BL, f"row_exp_in{i}", [BL], F32, S) for i in range(2)]
        at += 2 * BL
        roww_hi = [part(at + i * BL // 2, f"roww_hi{i}", [BL], F16, S) for i in range(2)]
        at += BL
        roww_lo = [part(at + i * BL // 2, f"roww_lo{i}", [BL], F16, S) for i in range(2)]
        at += BL
        assert at <= LOWER + UPPER

        bank = [ctx.enter_context(nc.psum_tensor(f"bank{i}", [P, 512], F32)) for i in range(8)]
        qk_ps = [bank[0][:, 0:BL], bank[1][:, 0:BL]]
        e_ps = [bank[2 + i][0:S, 0:BL] for i in range(4)]
        stat_ps = bank[6][0:S, 0:2 * S]
        factor_ps = bank[7][0:S, 0:S]
        colw_ps = [bank[i][0:S, 0:BL] for i in range(4)]
        col_ps = [bank[i][:, 0:BL] for i in range(4)]
        xt_ps = [bank[4][0:S, :], bank[5][0:S, :]]
        roww_ps = bank[6][0:S, 0:BL]
        row_ps = [bank[0][:, 0:BL], bank[1][:, 0:BL]]
        v_ps = [bank[2][:, 0:BL], bank[3][:, 0:BL]]

        SEED = 1
        s_const = sem("const_loaded")
        s_gamma = sem("gamma_loaded")
        s_id0 = sem("ident_cleared")
        s_id = sem("ident_ready")
        s_gbv = sem("gamma_bv_ready")
        s_whi = sem("weights_hi_ready")
        s_wlo = sem("weights_lo_ready")
        s_xin = [sem(f"x_loaded{i}") for i in range(XR)]
        s_early = [[sem(f"early_piece_loaded{g}_{i}") for i in range(XR, NP)] for g in range(1, CH)]
        s_xhi = sem("xr_hi_ready")
        s_xlo = sem("xr_lo_first_ready")
        s_xlo2 = sem("xr_lo_second_ready")
        s_amax = sem("x_amax_ready")
        s_qk = sem("qk_projected")
        s_qkev = sem("qk_evacuated")
        s_colqk = sem("qk_column_ready")
        s_qlow = sem("q_low_ready")
        s_klow = sem("k_low_ready")
        s_e = sem("energy_ready")
        s_nmax = sem("neg_max_ready")
        s_exp = sem("exp_ready")
        s_stat = sem("stats_kept")
        s_passed = sem("waits_passed")
        s_rstore = [sem(f"row_exp_stored{i}") for i in range(XR)]
        s_sall = sem("amax_all_ready")
        s_statT = sem("col_stats_transposed")
        s_dve = sem("dve_chain")
        s_fexp = sem("factor_exp_ready")
        s_fT = sem("col_factor_transposed")
        s_colf = sem("col_factor_ready")
        s_cw = sem("col_weight_ready")
        s_cwT = sem("col_weight_transposed")
        s_cwhi = sem("colw_hi_ready")
        s_cwlo = sem("colw_lo_ready")
        s_xchi = sem("xc_hi_ready")
        s_xclo = sem("xc_lo_ready")
        s_col = sem("col_average_ready")
        s_evA = sem("col_average_even_kept")
        s_evD = sem("col_average_odd_kept")
        s_spill = [sem(f"col_average_spilt{g}") for g in range(SPILT)]
        s_spin = [sem(f"spill_loaded{i}") for i in range(2)]
        s_rin = [sem(f"row_exp_loaded{i}") for i in range(2)]
        s_rw = sem("row_weight_ready")
        s_rwT = sem("row_weight_transposed")
        s_rwhi = sem("roww_hi_ready")
        s_rwlo = sem("roww_lo_ready")
        s_xT = sem("x_transposed")
        s_xthi = sem("xt_hi_ready")
        s_xtlo = sem("xt_lo_ready")
        s_row = sem("row_average_ready")
        s_av = sem("average_ready")
        s_avhi = sem("av_hi_ready")
        s_avlo = sem("av_lo_ready")
        s_v = sem("value_ready")
        s_out = sem("output_ready")
        s_store = [sem(f"output_stored{i}") for i in range(XR)]

        AMAX_AT, SCALE_AT, MAX_AT, COL_FACTOR_AT, CHAIN = 1, 6, 10, 16, 17

        COLS_FIRST = [NB] + [NB + NP + (g - 1) * XR for g in range(1, CH)]
        OUT_FIRST = NB + NP + (CH - 1) * XR
        XPI = OUT_FIRST + NB
        LPS = XPI // XR

        def x_loaded(eng, n, first, b, k):
            eng.wait_ge(s_xin[k % XR], 16 * (n * LPS + first // XR + (b - k % XR) // XR + 1)
                        if isinstance(b, int) else (n * LPS + first // XR + 1) * 16 + (b - k % XR) * (16 // XR))

        def piece_of(g, i, k):
            if g >= 1 and i >= XR:
                return early[:, (g + 1) % KEPT, i - XR, :, :]
            return x_ring[0:S, k % XR, :].rearrange("p (c n) -> p c n", c=CP)

        def slot_stored(eng, sems, n, b, k):
            eng.wait_ge(sems[k % XR], 16 * SEED + n * (16 * NB // XR) + (b - k % XR) * (16 // XR))

        def all_stored(eng, sems, n):
            for s in sems:
                eng.wait_ge(s, 16 * SEED + n * (16 * NB // XR))

        def alone(eng):
            eng.sem_inc(s_passed, 1)

        block = ctx.enter_context(nc.Block())

        @block.sync
        def _(sp):
            sp.dma_start(gamma_sb[:, :], gamma).then_inc(s_gamma, 16)
            sp.dma_start(x_ring[:, 0:2, :].rearrange("p s n -> p (s n)")[:, 0:CH * C].rearrange("p (c n) -> p c n", c=CH),
                         wvT.rearrange("(c p) n -> p c n", p=P)).then_inc(s_const, 16)
            sp.dma_start(x_ring[:, 2, 0:CH * P].rearrange("p (c n) -> p c n", c=CH),
                         wqkT.rearrange("(c p) n -> p c n", p=P)).then_inc(s_const, 16)
            sp.dma_start(bqk_sb[:, :], bqk).then_inc(s_const, 16)
            sp.dma_start(bv_sb[:, :], bv).then_inc(s_const, 16)
            for s in (*s_rstore, *s_store):
                sp.sem_inc(s, 16 * SEED)
            sp.wait_ge(s_wlo, 2)

            def load_rows(n, b, k):
                sp.dma_start(x_ring[:, k % XR, :].rearrange("p (c n) -> p c n", c=CH),
                             x_rows[n, b]).then_inc(s_xin[k % XR], 16)

            def load_cols(n, i, k):
                sp.dma_start(x_ring[0:S, k % XR, :].rearrange("p (c n) -> p c n", c=CP),
                             x_cols[n, i]).then_inc(s_xin[k % XR], 16)

            def image(n, more):
                def rows_step(t, k):
                    if XR <= k < NB + XR:
                        sp.wait_ge(s_xlo, n * NB + t - (XR - 1))
                        sp.wait_ge(s_xlo2, n * NB + t - (XR - 1))
                        sp.wait_ge(s_amax, n * NB + t - (XR - 1))
                        alone(sp)
                        if inside(k):
                            load_rows(n, t, k)
                        else:
                            load_cols(n, t - NB, k)
                    if inside(k - 8):
                        sp.wait_ge(s_exp, n * (2 * NB) + t - 7)
                        sp.dma_start(row_exp_dram[:, t - 8, :],
                                     row_exp[k % 4][:, :, :].rearrange("p l n -> p (l n)")).then_inc(s_rstore[k % 4], 16)

                walk(sp, rows_step, 8, 2 * XR)

                def load_piece(g, i, before):
                    sp.wait_ge(s_xclo, n * (CH * NP) + before)
                    load_cols(n, g * NP + i, i)

                def load_early(g):
                    for i in range(XR, NP):
                        sp.dma_start(piece_of(g, i, i), x_cols[n, g * NP + i]).then_inc(s_early[g - 1][i - XR], 16)

                def spill(g):
                    sp.wait_ge(s_evA, SEED + n * (CH * NB // 2) + (g + 1) * (NB // 2))
                    sp.wait_ge(s_evD, SEED + n * (CH * NB // 2) + (g + 1) * (NB // 2))
                    sp.dma_start(spill_dram[g], kept[:, (g + 1) % KEPT, :]).then_inc(s_spill[g], 16)

                for i in range(XR, NP):
                    load_piece(0, i, i - XR + 1)
                for i in range(XR):
                    load_piece(1, i, NP - XR + i + 1)
                sp.wait_ge(s_colqk, (n + 1) * NB)
                alone(sp)
                load_early(1)
                for g in range(2, CH):
                    spill(g - 2)
                    for i in range(XR):
                        load_piece(g, i, (g - 1) * NP + i + 1)
                    sp.wait_ge(s_spill[g - 2], n * 16 + 16)
                    alone(sp)
                    load_early(g)

                for b in range(XR):
                    sp.wait_ge(s_xclo, n * (CH * NP) + (CH - 1) * NP + 1 + b)
                    load_rows(n, b, b)

                def out_step(t, k):
                    if inside(k):
                        if k >= XR:
                            slot_stored(sp, s_store, n, t, k)
                            load_rows(n, t, k)
                        if k == 0:
                            sp.wait_ge(s_col, SEED + (n + 1) * (CH * NB))
                            alone(sp)
                            for s in s_spill:
                                sp.wait_ge(s, n * 16 + 16)
                                alone(sp)
                            all_stored(sp, s_rstore, n + 1)
                        if k >= 2:
                            sp.wait_ge(s_rw, n * NB + t - 1)
                            alone(sp)
                        sp.dma_start(row_exp_in[k % 2][:, :], row_exp_dram[:, t, :]).then_inc(s_rin[k % 2], 16)
                        if k >= 2:
                            sp.wait_ge(s_av, n * (CH * NB) + t * CH - CH)
                        sp.dma_start(spill_in[k % 2][:, :, :], spill_dram.rearrange("c p (b n) -> b p c n", n=BL)[t])\
                            .then_inc(s_spin[k % 2], 16)
                    if inside(k - 3):
                        sp.wait_ge(s_out, n * (CH * NB) + t * CH - 2 * CH)
                        sp.dma_start(out_rows[n, t - 3],
                                     x_ring[:, (k - 3) % XR, :].rearrange("p (c n) -> p c n", c=CH))\
                            .then_inc(s_store[(k - 3) % XR], 16)
                    if k >= NB and more:
                        sp.wait_ge(s_store[k - NB], 16 * SEED + (n + 1) * (16 * NB // XR))
                        load_rows(n + 1, k - NB, k)

                walk(sp, out_step, 4)

            for b in range(XR):
                load_rows(0, b, b)
            with sp.Fori(0, N - 1) as n:
                image(n, True)
            image(N - 1, False)
            all_stored(sp, s_store, N)

        @block.gpsimd
        def _(pool):
            pool.memset(ident[:, :], 0.0).then_inc(s_id0, 1)
            pool.memset(ident_bf[:, :], 0.0).then_inc(s_id0, 1)
            pool.memset(neg_diag[:, :, :], 0.0).then_inc(s_id0, 1)
            pool.wait_ge(s_id0, 3)
            pool.affine_select(out=ident[:, :], in_=ident[:, :], compare_op=ALU.not_equal, fill=1.0, base=0,
                               pattern=[[-1, P]], channel_multiplier=1).then_inc(s_id, 1)
            pool.affine_select(out=ident_bf[:, :], in_=ident_bf[:, :], compare_op=ALU.not_equal, fill=1.0, base=0,
                               pattern=[[-1, S]], channel_multiplier=1).then_inc(s_id, 1)
            pool.affine_select(out=neg_diag[:, :, :], in_=neg_diag[:, :, :], compare_op=ALU.not_equal, fill=NEG,
                               base=0, pattern=[[0, L], [-1, S]], channel_multiplier=1).then_inc(s_id, 1)
            with pool.Fori(0, N) as n:
                def rows_step(t, k):
                    if inside(k):
                        x_loaded(pool, n, 0, t, k)
                        pool.wait_ge(s_xhi, n * NB + t + 1)
                        pool.tensor_tensor(xr_lo[k % 4][:, 0:POOL_CH, :].rearrange("p c n -> p (c n)"),
                                           x_ring[:, k % XR, 0:POOL_CH * BL],
                                           xr_hi[k % 4][:, 0:POOL_CH, :].rearrange("p c n -> p (c n)").bitcast(F32),
                                           ALU.subtract).then_inc(s_xlo, 1)

                walk(pool, rows_step, 0)

                pool.wait_ge(s_dve, n * CHAIN + AMAX_AT)
                alone(pool)
                pool.partition_all_reduce(amax_all, amax1, P, bass.bass_isa.ReduceOp.max).then_inc(s_sall, 1)

                qk_by_col = qk_all.rearrange("p (y x) -> p x y", x=S)
                pool.wait_ge(s_qkev, (n + 1) * NB)
                alone(pool)

                def cols_step(t, k, j):
                    pool.wait_ge(s_e, n * (2 * NB) + NB + t - 3)
                    alone(pool)
                    pool.tensor_copy(qk_col[k % 4][:, :].rearrange("p (l y) -> p l y", l=L),
                                     qk_by_col[:, bass.ds(t * L, L), :]).then_inc(s_colqk, 1)

                loop(pool, cols_step, XR)

                pool.wait_ge(s_colf, n + 1)
                col_exp3 = col_exp.rearrange("p (x y) -> p x y", y=S)

                def colw_step(t, k):
                    if k >= 4:
                        pool.wait_ge(s_cwT, n * NB + t - 3)
                    pool.tensor_tensor(col_weight[:, k % 4, :].rearrange("p (l n) -> p l n", l=L),
                                       col_exp3[:, bass.ds(t * L, L), :],
                                       col_factor[:, bass.ds(t * L, L)].unsqueeze(2).to_broadcast([S, L, S]),
                                       ALU.mult).then_inc(s_cw, 1)

                walk(pool, colw_step, 0)

                pool.wait_ge(s_dve, (n + 1) * CHAIN)

                def out_step(t, k):
                    if inside(k):
                        pool.wait_ge(s_rin[k % 2], n * (8 * NB) + (t - k % 2) * 8 + 16)
                        if k >= 2:
                            pool.wait_ge(s_rwT, n * NB + t - 1)
                        pool.tensor_tensor(weight[:, k % 2, :].rearrange("p (l n) -> p l n", l=L),
                                           row_exp_in[k % 2][:, :].rearrange("p (l n) -> p l n", l=L),
                                           row_factor[:, bass.ds(t * L, L)].unsqueeze(2).to_broadcast([S, L, S]),
                                           ALU.mult).then_inc(s_rw, 1)
                    if inside(k - 2):
                        for c in range(CH):
                            pool.wait_ge(s_avhi, n * (CH * NB) + (t - 2) * CH + c + 1)
                            pool.tensor_tensor(av_lo[k % 2][:, c, :], av[:, c, :],
                                               av_hi[k % 2][:, c, :].bitcast(F32), ALU.subtract).then_inc(s_avlo, 1)

                walk(pool, out_step, 2)

        @block.scalar
        def _(act):
            act.wait_ge(s_gamma, 16)
            act.wait_ge(s_const, 64)
            wv_in = x_ring[:, 0:2, :].rearrange("p s n -> p (s n)")[:, 0:CH * C].rearrange("p (c n) -> p c n", c=CH)
            wqk_in = x_ring[:, 2, 0:CH * P].rearrange("p (c n) -> p c n", c=CH)
            act.activation(wv_hi[:, :, :], wv_in, ACT.Copy, scale=gamma_sb[:, 0:1]).then_inc(s_whi, 1)
            act.activation(wqk_hi[:, :, :], wqk_in, ACT.Copy).then_inc(s_whi, 1)
            with act.Fori(0, N) as n:
                def exps(t, k, first, dest):
                    act.wait_ge(s_nmax, n * (2 * NB) + first + t + 1)
                    for r in range(L):
                        last = act.activation(dest[:, r, :], e_ps[k % 4][:, r * S:(r + 1) * S], ACT.Exp,
                                              bias=neg_max[:, k % 4, r:r + 1], accum_out=exp_sum[:, k % 4, r:r + 1])
                    last.then_inc(s_exp, 1)

                def rows_step(t, k):
                    if inside(k):
                        x_loaded(act, n, 0, t, k)
                        if k >= 4:
                            act.wait_ge(s_qk, n * NB + t - 3)
                        act.activation(xr_hi[k % 4][:, :, :].rearrange("p c n -> p (c n)"), x_ring[:, k % XR, :],
                                       ACT.Copy).then_inc(s_xhi, 1)
                    if inside(k - 2):
                        act.wait_ge(s_qk, n * NB + t - 1)
                        act.activation(qk_all[:, bass.ds((t - 2) * BL, BL)], qk_ps[k % 2], ACT.Identity,
                                       bias=bqk_sb[:, 0:1]).then_inc(s_qkev, 1)
                    if inside(k - 5):
                        if k - 5 >= 4:
                            slot_stored(act, s_rstore, n, t - 5, k - 5)
                            act.wait_ge(s_stat, n * (2 * NB) + t - 8)
                        exps(t - 5, k - 5, 0, row_exp[(k - 5) % 4][:, :, :])

                walk(act, rows_step, 5, 3 * XR)

                col_exp3 = col_exp.rearrange("p (x y) -> p x y", y=S)

                def split_piece(g, i, k):
                    if g >= 1 and i >= XR:
                        act.wait_ge(s_early[g - 1][i - XR], n * 16 + 16)
                    else:
                        x_loaded(act, n, COLS_FIRST[g], i, k)
                    act.activation(xc_hi[:, :, bass.ds(i * CP, CP)].rearrange("p x c -> p c x"),
                                   piece_of(g, i, k), ACT.Copy,
                                   scale=x_scale[0:S, :]).then_inc(s_xchi, 1)

                act.wait_ge(s_dve, n * CHAIN + SCALE_AT)

                def cols_step(t, k, j):
                    if k % PS == 0:
                        split_piece(0, j * XR + k // PS, k // PS)
                    act.wait_ge(s_stat, n * (2 * NB) + NB + t - 3)
                    exps(t, k, NB, col_exp3[:, bass.ds(t * L, L), :])

                loop(act, cols_step, PS * XR)

                act.wait_ge(s_dve, n * CHAIN + MAX_AT)
                act.activation(row_nmax, row_nmax, ACT.Exp).then_inc(s_fexp, 1)
                act.activation(row_factor[:, :], row_factor[:, :], ACT.Exp).then_inc(s_fexp, 1)

                all_stored(act, s_rstore, n + 1)

                def colw_step(t, k):
                    act.wait_ge(s_cwT, n * NB + t + 1)
                    act.activation(colw_hi[:, bass.ds(t * L, L), :],
                                   colw_ps[k % 4].rearrange("p (l n) -> p l n", l=L), ACT.Copy).then_inc(s_cwhi, 1)

                walk(act, colw_step, 0)

                for g in range(CH):
                    if g >= KEPT:
                        act.wait_ge(s_spill[g - KEPT], n * 16 + 16)
                    kept_by_col = kept[:, (g + 1) % KEPT, :].rearrange("p (y x) -> p x y", x=S)
                    with act.Fori(0, NB // 4) as j:
                        for u in (0, 2):
                            act.wait_ge(s_col, SEED + n * (CH * NB) + g * NB + j * 4 + u + 1)
                            act.activation(kept_by_col[:, bass.ds(j * (4 * L) + u * L, L), :],
                                           col_ps[u].rearrange("p (l n) -> p l n", l=L), ACT.Copy,
                                           scale=x_unscale).then_inc(s_evA, 1)
                    if g < CH - 1:
                        act.wait_ge(s_col, SEED + n * (CH * NB) + (g + 1) * NB)
                        for i in range(NP):
                            split_piece(g + 1, i, i)

                def row_weights(t, k):
                    act.wait_ge(s_rwT, n * NB + t + 1)
                    act.activation(roww_hi[k % 2][:, :], roww_ps, ACT.Copy).then_inc(s_rwhi, 1)

                act.wait_ge(s_col, SEED + (n + 1) * (CH * NB))

                def out_step(t, k):
                    if inside(k):
                        if k >= 2:
                            act.wait_ge(s_row, n * (CH * NB) + t * CH - CH)
                        if k >= 1:
                            row_weights(t, k)
                    for r in range(4):
                        if inside(k):
                            act.wait_ge(s_xT, n * (L * NB) + t * L + r + 1)
                            act.activation(xt_hi[k % 2][:, r, :], xt_ps[r % 2], ACT.Copy,
                                           scale=x_scale[0:S, :]).then_inc(s_xthi, 1)
                        if inside(k - 1):
                            act.wait_ge(s_av, n * (CH * NB) + (t - 1) * CH + r + 1)
                            if k - 1 >= 2 and r == 0:
                                act.wait_ge(s_v, SEED + n * (CH * NB) + (t - 2) * CH)
                            act.activation(av_hi[(k - 1) % 2][:, r, :], av[:, r, :], ACT.Copy).then_inc(s_avhi, 1)
                    if k == 0:
                        row_weights(t, k)

                walk(act, out_step, 1)

        @block.vector
        def _(dve):
            wv_in = x_ring[:, 0:2, :].rearrange("p s n -> p (s n)")[:, 0:CH * C].rearrange("p (c n) -> p c n", c=CH)
            wqk_in = x_ring[:, 2, 0:CH * P].rearrange("p (c n) -> p c n", c=CH)
            dve.wait_ge(s_const, 64)
            dve.wait_ge(s_gamma, 16)
            dve.tensor_scalar(gbv[:, :], bv_sb[:, :], gamma_sb[:, 0:1], None, ALU.mult).then_inc(s_gbv, 1)
            dve.wait_ge(s_gbv, 1)
            dve.wait_ge(s_whi, 2)
            dve.scalar_tensor_tensor(out=wv_lo[:, :, :], in0=wv_in, scalar=gamma_sb[:, 0:1],
                                     in1=wv_hi[:, :, :].bitcast(F32), op0=ALU.mult,
                                     op1=ALU.subtract).then_inc(s_wlo, 1)
            dve.tensor_tensor(wqk_lo[:, :, :], wqk_in, wqk_hi[:, :, :].bitcast(F32), ALU.subtract).then_inc(s_wlo, 1)
            with dve.Fori(0, N) as n:
                def line_max(b, k):
                    dve.wait_ge(s_e, n * (2 * NB) + b + 1)
                    if k >= 4:
                        dve.wait_ge(s_stat, n * (2 * NB) + b - 3)
                    dve.tensor_reduce(neg_max[:, k % 4, :], e_ps[k % 4].rearrange("p (l n) -> p l n", l=L), AX.X,
                                      ALU.max, negate=True).then_inc(s_nmax, 1)

                def keep_stats(b, k):
                    dve.wait_ge(s_exp, n * (2 * NB) + b + 1)
                    dve.tensor_copy(stats[:, :, bass.ds(b * L, L)], block_stats[:, k % 4, :, :]).then_inc(s_stat, 1)

                def rows_step(t, k):
                    if inside(k):
                        x_loaded(dve, n, 0, t, k)
                        dve.wait_ge(s_xhi, n * NB + t + 1)
                        dve.tensor_tensor(xr_lo[k % 4][:, POOL_CH:CH, :].rearrange("p c n -> p (c n)"),
                                          x_ring[:, k % XR, POOL_CH * BL:CH * BL],
                                          xr_hi[k % 4][:, POOL_CH:CH, :].rearrange("p c n -> p (c n)").bitcast(F32),
                                          ALU.subtract).then_inc(s_xlo2, 1)
                        dve.tensor_reduce(x_amax[:, bass.ds(t, 1)], x_ring[:, k % XR, :], AX.X, ALU.max,
                                          apply_absolute_value=True).then_inc(s_amax, 1)
                    if inside(k - 2):
                        dve.wait_ge(s_qkev, n * NB + t - 1)
                        if k - 2 >= 2:
                            dve.wait_ge(s_e, n * (2 * NB) + t - 3)
                        dve.tensor_copy(q_low[k % 2][:, :], qk_all[0:CQ, bass.ds((t - 2) * BL, BL)]).then_inc(s_qlow, 1)
                        dve.tensor_copy(k_low[k % 2][:, :],
                                        qk_all[CQ:2 * CQ, bass.ds((t - 2) * BL, BL)]).then_inc(s_klow, 1)
                    if inside(k - 4):
                        line_max(t - 4, k - 4)
                    if inside(k - 6):
                        keep_stats(t - 6, k - 6)

                walk(dve, rows_step, 2, 3 * XR)

                done = [0]

                def chain(ins):
                    done[0] += 1
                    ins.then_inc(s_dve, 1)
                    dve.wait_ge(s_dve, n * CHAIN + done[0])

                dve.wait_ge(s_amax, (n + 1) * NB)
                chain(dve.tensor_reduce(amax1, x_amax[:, :], AX.X, ALU.max))
                assert done[0] == AMAX_AT
                dve.wait_ge(s_sall, n + 1)
                chain(dve.tensor_scalar(amax_all, amax_all, TINY, None, ALU.max))
                chain(dve.tensor_scalar(power.bitcast(U32), amax_all.bitcast(U32), EXPONENT, None, ALU.bitwise_and))
                chain(dve.tensor_scalar(x_scale.bitcast(U32), amax_all.bitcast(U32), EXPONENT, EXPONENT,
                                        ALU.bitwise_xor, ALU.bitwise_and))
                chain(dve.tensor_scalar(x_unscale, power, 0.5 / (X_SCALE * P_SCALE), None, ALU.mult))
                chain(dve.tensor_scalar(x_scale, x_scale, X_SCALE, None, ALU.mult))
                assert done[0] == SCALE_AT

                def split_piece(g, i, k):
                    dve.wait_ge(s_xchi, n * (CH * NP) + g * NP + i + 1)
                    cols = xc_lo[:, :, bass.ds(i * CP, CP)], xc_hi[:, :, bass.ds(i * CP, CP)]
                    lo, hi = (v.rearrange("p x c -> p c x") for v in cols)
                    dve.scalar_tensor_tensor(out=lo, in0=piece_of(g, i, k),
                                             scalar=x_scale[0:S, :], in1=hi, op0=ALU.mult,
                                             op1=ALU.subtract).then_inc(s_xclo, 1)

                def column_k(t, k):
                    dve.wait_ge(s_colqk, n * NB + t + 1)
                    dve.wait_ge(s_e, n * (2 * NB) + NB + t - 3)
                    dve.tensor_copy(k_col[k % 4][:, :], qk_col[k % 4][CQ:2 * CQ, :]).then_inc(s_klow, 1)

                def cols_step(t, k, j):
                    if k == 0:
                        column_k(t, k)
                    if k < PS * XR - 1:
                        column_k(t + 1, k + 1)
                    if k > 0:
                        line_max(NB + t - 1, 12 + k - 1)
                    keep_stats(NB + t - 3, 12 + k - 3)
                    if k == PS * XR - 1:
                        line_max(NB + t, 12 + k)
                    if k % PS == PS - 1:
                        split_piece(0, j * XR + k // PS, k // PS)

                line_max(NB - 2, NB - 2)
                keep_stats(NB - 4, NB - 4)
                line_max(NB - 1, NB - 1)
                alone(dve)
                loop(dve, cols_step, PS * XR)
                for b in range(2 * NB - 3, 2 * NB):
                    keep_stats(b, b)

                dve.wait_ge(s_stat, (n + 1) * (2 * NB))
                dve.wait_ge(s_statT, n + 1)
                joint = weight[:, 0, 0:S]
                col_sumT = weight[:, 0, S:2 * S]
                chain(dve.tensor_tensor(joint, stat_ps[:, 0:S], row_nmax, ALU.min))
                chain(dve.tensor_copy(col_sumT, stat_ps[:, S:2 * S]))
                chain(dve.tensor_tensor(row_nmax, joint, row_nmax, ALU.subtract))
                chain(dve.tensor_tensor(row_factor[:, :], joint, stat_ps[:, 0:S], ALU.subtract))
                assert done[0] == MAX_AT
                dve.wait_ge(s_fexp, 2 * n + 2)
                chain(dve.tensor_tensor(row_sum, row_sum, row_nmax, ALU.mult))
                chain(dve.tensor_tensor(col_sumT, col_sumT, row_factor[:, :], ALU.mult))
                chain(dve.tensor_tensor(joint, row_sum, col_sumT, ALU.add))
                chain(dve.reciprocal(joint, joint))
                chain(dve.tensor_scalar(joint, joint, P_SCALE, None, ALU.mult))
                chain(dve.tensor_tensor(col_sumT, row_factor[:, :], joint, ALU.mult))
                assert done[0] == COL_FACTOR_AT
                chain(dve.tensor_tensor(row_factor[:, :], row_nmax, joint, ALU.mult))
                assert done[0] == CHAIN
                dve.wait_ge(s_fT, n + 1)
                dve.tensor_copy(col_factor[:, :], factor_ps).then_inc(s_colf, 1)

                def colw_step(t, k):
                    dve.wait_ge(s_cwhi, n * NB + t + 1)
                    dve.tensor_tensor(colw_lo[:, bass.ds(t * L, L), :],
                                      colw_ps[k % 4].rearrange("p (l n) -> p l n", l=L),
                                      colw_hi[:, bass.ds(t * L, L), :], ALU.subtract).then_inc(s_cwlo, 1)

                walk(dve, colw_step, 0)

                for g in range(CH):
                    if g >= KEPT:
                        dve.wait_ge(s_spill[g - KEPT], n * 16 + 16)
                        alone(dve)
                    kept_by_col = kept[:, (g + 1) % KEPT, :].rearrange("p (y x) -> p x y", x=S)
                    with dve.Fori(0, NB // 4) as j:
                        for u in (1, 3):
                            dve.wait_ge(s_col, SEED + n * (CH * NB) + g * NB + j * 4 + u + 1)
                            dve.tensor_scalar(kept_by_col[:, bass.ds(j * (4 * L) + u * L, L), :],
                                              col_ps[u].rearrange("p (l n) -> p l n", l=L), x_unscale, None,
                                              ALU.mult).then_inc(s_evD, 1)
                    if g < CH - 1:
                        for i in range(NP):
                            split_piece(g + 1, i, i)

                dve.wait_ge(s_evA, SEED + (n + 1) * (CH * NB // 2))

                def row_weights(t, k):
                    dve.wait_ge(s_rwhi, n * NB + t + 1)
                    dve.tensor_tensor(roww_lo[k % 2][:, :], roww_ps, roww_hi[k % 2][:, :],
                                      ALU.subtract).then_inc(s_rwlo, 1)

                def out_step(t, k):
                    if 1 <= k < NB:
                        row_weights(t, k)
                    for r in range(4):
                        if inside(k):
                            dve.wait_ge(s_xthi, n * (L * NB) + t * L + r + 1)
                            dve.scalar_tensor_tensor(out=xt_lo[k % 2][:, r, :], in0=xt_ps[r % 2],
                                                     scalar=x_scale[0:S, :], in1=xt_hi[k % 2][:, r, :],
                                                     op0=ALU.mult, op1=ALU.subtract).then_inc(s_xtlo, 1)
                        if inside(k - 1):
                            dve.wait_ge(s_row, n * (CH * NB) + (t - 1) * CH + r + 1)
                            if k - 1 >= 1:
                                dve.wait_ge(s_avlo, n * (CH * NB) + (t - 2) * CH + r + 1)
                            if r < SPILT:
                                if r == 0:
                                    dve.wait_ge(s_spin[(k - 1) % 2], n * (8 * NB) + (t - 1 - (k - 1) % 2) * 8 + 16)
                                col = spill_in[(k - 1) % 2][:, r, :]
                            else:
                                col = kept[:, (r + 1) % KEPT, bass.ds((t - 1) * BL, BL)]
                            dve.scalar_tensor_tensor(out=av[:, r, :], in0=row_ps[r % 2], scalar=x_unscale, in1=col,
                                                     op0=ALU.mult, op1=ALU.add).then_inc(s_av, 1)
                        if inside(k - 2):
                            dve.wait_ge(s_v, SEED + n * (CH * NB) + (t - 2) * CH + r + 1)
                            res = x_ring[:, (k - 2) % XR, r * BL:(r + 1) * BL]
                            dve.scalar_tensor_tensor(out=res, in0=v_ps[r % 2], scalar=gbv[:, r:r + 1], in1=res,
                                                     op0=ALU.add, op1=ALU.add).then_inc(s_out, 1)
                    if k == 0:
                        row_weights(t, k)

                walk(dve, out_step, 2)

        @block.tensor
        def _(pe):
            for s in (s_v, s_col, s_evA, s_evD):
                pe.sem_inc(s, SEED)
            pe.wait_ge(s_id, 3)
            pe.wait_ge(s_wlo, 2)
            with pe.Fori(0, N) as n:
                def energies(t, k, first, masked, q, kk):
                    pe.wait_ge(s_klow, n * (2 * NB) + first + t + 1)
                    if k >= 4 or first:
                        pe.wait_ge(s_exp, n * (2 * NB) + first + t - 3)
                    if masked:
                        pe.matmul(e_ps[k % 4], ident_bf[:, :], neg_diag[:, :, :].rearrange("p l n -> p (l n)"),
                                  start=True, stop=False)
                    for r in range(L):
                        line = slice(r * S, (r + 1) * S)
                        last = pe.matmul(e_ps[k % 4][:, line], q[0:CQ, line], kk[:, line],
                                         start=not masked, stop=not masked or r == L - 1)
                    last.then_inc(s_e, 1)

                def rows_step(t, k):
                    if inside(k):
                        pe.wait_ge(s_xlo, n * NB + t + 1)
                        pe.wait_ge(s_xlo2, n * NB + t + 1)
                        if k >= 2:
                            pe.wait_ge(s_qkev, n * NB + t - 1)
                        for c in range(CH):
                            for i, (w, m) in enumerate(((wqk_hi, xr_hi), (wqk_lo, xr_hi), (wqk_hi, xr_lo))):
                                last = pe.matmul(qk_ps[k % 2], w[:, c, :], m[k % 4][:, c, :],
                                                 start=c == 0 and i == 0, stop=c == CH - 1 and i == 2)
                        last.then_inc(s_qk, 1)
                    if inside(k - 2):
                        pe.wait_ge(s_qlow, n * NB + t - 1)
                        energies(t - 2, k - 2, 0, False, q_low[k % 2], k_low[k % 2])

                walk(pe, rows_step, 2)

                def cols_step(t, k, j):
                    energies(t, k, NB, True, qk_col[k % 4], k_col[k % 4])

                loop(pe, cols_step, XR)

                pe.wait_ge(s_stat, (n + 1) * (2 * NB))
                pe.transpose(stat_ps[:, 0:S], col_nmax, ident[0:S, 0:S])
                pe.transpose(stat_ps[:, S:2 * S], col_sum, ident[0:S, 0:S]).then_inc(s_statT, 1)
                pe.wait_ge(s_dve, n * CHAIN + COL_FACTOR_AT)
                pe.transpose(factor_ps, weight[:, 0, S:2 * S], ident[0:S, 0:S]).then_inc(s_fT, 1)

                def colw_step(t, k):
                    pe.wait_ge(s_cw, n * NB + t + 1)
                    if k >= 4:
                        pe.wait_ge(s_cwlo, n * NB + t - 3)
                    for r in range(L):
                        line = slice(r * S, (r + 1) * S)
                        last = pe.transpose(colw_ps[k % 4][:, line], col_weight[:, k % 4, line], ident[0:S, 0:S])
                    last.then_inc(s_cwT, 1)

                walk(pe, colw_step, 0)

                pe.wait_ge(s_cwlo, (n + 1) * NB)
                alone(pe)
                with pe.Fori(0, CH) as g:
                    pe.wait_ge(s_xclo, n * (CH * NP) + g * NP + NP)
                    pe.wait_ge(s_evA, SEED + n * (CH * NB // 2) + g * (NB // 2))
                    pe.wait_ge(s_evD, SEED + n * (CH * NB // 2) + g * (NB // 2))
                    for b in range(NB):
                        if b >= 4:
                            read = s_evA if b % 2 == 0 else s_evD
                            pe.wait_ge(read, SEED + n * (CH * NB // 2) + g * (NB // 2) + (b - 4) // 2 + 1)
                        for r in range(L):
                            col = b * L + r
                            for i, (w, m) in enumerate(((xc_hi, colw_hi), (xc_hi, colw_lo), (xc_lo, colw_hi))):
                                last = pe.matmul(col_ps[b % 4][:, r * S:(r + 1) * S], w[:, col, :], m[:, col, :],
                                                 start=i == 0, stop=i == 2)
                        last.then_inc(s_col, 1)

                def row_weights(t, k):
                    pe.wait_ge(s_rw, n * NB + t + 1)
                    if k >= 1:
                        pe.wait_ge(s_rwlo, n * NB + t)
                    for r in range(L):
                        line = slice(r * S, (r + 1) * S)
                        last = pe.transpose(roww_ps[:, line], weight[:, k % 2, line], ident[0:S, 0:S])
                    last.then_inc(s_rwT, 1)

                def out_step(t, k):
                    if inside(k):
                        if k >= 1:
                            row_weights(t, k)
                        x_loaded(pe, n, OUT_FIRST, t, k)
                    for r in range(4):
                        if inside(k):
                            if k >= 1 or r >= 2:
                                pe.wait_ge(s_xtlo, n * (L * NB) + t * L + r - 1)
                            for c in range(CH):
                                last = pe.transpose(xt_ps[r % 2][:, c * P:(c + 1) * P],
                                                    x_ring[:, k % XR, c * BL + r * S:c * BL + (r + 1) * S],
                                                    ident[:, :])
                            last.then_inc(s_xT, 1)
                        if inside(k - 1):
                            s = (k - 1) % 2
                            if r == 0:
                                pe.wait_ge(s_xtlo, n * (L * NB) + t * L)
                                pe.wait_ge(s_rwlo, n * NB + t)
                            if k - 1 >= 1 or r >= 2:
                                pe.wait_ge(s_av, n * (CH * NB) + (t - 1) * CH + r - 1)
                            for row in range(L):
                                line = slice(row * S, (row + 1) * S)
                                for i, (w, m) in enumerate(((xt_hi, roww_hi), (xt_hi, roww_lo), (xt_lo, roww_hi))):
                                    last = pe.matmul(row_ps[r % 2][:, line], w[s][:, row, r * P:(r + 1) * P],
                                                     m[s][:, line], start=i == 0, stop=i == 2)
                            last.then_inc(s_row, 1)
                        if inside(k - 2):
                            s = (k - 2) % 2
                            if k - 2 >= 1 or r >= 2:
                                pe.wait_ge(s_out, n * (CH * NB) + (t - 2) * CH + r - 1)
                            for c in range(CH):
                                if r == 0:
                                    pe.wait_ge(s_avlo, n * (CH * NB) + (t - 2) * CH + c + 1)
                                for i, (w, m) in enumerate(((wv_hi, av_hi), (wv_lo, av_hi), (wv_hi, av_lo))):
                                    last = pe.matmul(v_ps[r % 2], w[:, c, r * P:(r + 1) * P], m[s][:, c, :],
                                                     start=c == 0 and i == 0, stop=c == CH - 1 and i == 2)
                            last.then_inc(s_v, 1)
                    if k == 0:
                        row_weights(t, k)

                walk(pe, out_step, 2)


def kernel(**inputs):
    import numpy as _np
    import concourse.bacc as _bacc
    from concourse import mybir as _mybir
    from concourse.bass_utils import run_bass_kernel_spmd as _run

    laid = {
        "x": _np.ascontiguousarray(inputs["x"]),
        "wqkT": _np.ascontiguousarray(_np.concatenate([inputs["L0_conv_wq"], inputs["L0_conv_wk"]], axis=0).T),
        "bqk": _np.concatenate([inputs["L0_conv_bq"], inputs["L0_conv_bk"]]).reshape(P, 1),
        "wvT": _np.ascontiguousarray(_np.asarray(inputs["L0_conv_wv"]).T),
        "bv": _np.ascontiguousarray(_np.asarray(inputs["L0_conv_bv"]).reshape(CH, P).T),
        "gamma": _np.ascontiguousarray(_np.broadcast_to(_np.asarray(inputs["L0_conv_gamma"]), (P, 1))),
    }
    nc = _bacc.Bacc("TRN2", target_bir_lowering=False, num_devices=1)
    arrays, args = {}, []
    for name, a in laid.items():
        arrays[f"in_{name}"] = a
        args.append(nc.dram_tensor(f"in_{name}", a.shape, _mybir.dt.from_np(a.dtype), kind="ExternalInput").ap())
    args.append(nc.dram_tensor("out_0", (N, C, H, W), _mybir.dt.float32, kind="ExternalOutput").ap())
    criss_cross(nc, *args)
    r = _run(nc, [arrays], core_ids=[0])
    return r.results[0]["out_0"]
```
